# Optimizing a Trainium2 kernel written in Bass

```python
import numpy as np
import jax
import jax.numpy as jnp

def _softmax(x, axis=-1):
    return jax.nn.softmax(x, axis=axis)

def _gelu(x):
    return jax.nn.gelu(x, approximate=True)

def _silu(x):
    return jax.nn.silu(x)

def _sigmoid(x):
    return jax.nn.sigmoid(x)

def _layernorm(x, axis=-1, eps=1e-05):
    m = jnp.mean(x, axis=axis, keepdims=True)
    v = jnp.var(x, axis=axis, keepdims=True)
    return (x - m) / jnp.sqrt(v + eps)

def _scatter_add(tgt, idx, src, axis=0):
    return tgt.at[idx].add(src)

def _segment_sum(src, seg, n):
    return jax.ops.segment_sum(src, seg, n)
kernel_name = 'mk_xattn_ffn_d2_seqx_r8_1f18a5'

def setup_inputs(seed: int=0):
    np.random.seed(seed)
    _w = jnp.asarray

    def _rec_inputs():
        import jax
        import jax.numpy as jnp
        _rk = jax.random.key(seed)
        x = 7.22e-05 + 1 * jax.random.normal(jax.random.fold_in(_rk, 1), (8, 128, 128), jnp.float32)
        _lenS = 128 - jax.random.randint(jax.random.fold_in(_rk, 7), (8,), 0, max(1, 128 // 4) + 1, jnp.int32)
        _lenS2 = 128 - jax.random.randint(jax.random.fold_in(_rk, 8), (8,), 0, max(1, 128 // 4) + 1, jnp.int32)
        _ctx_768P = jax.random.normal(jax.random.fold_in(_rk, 11), (8, 16, 96), jnp.float32)
        _ctx_768c = jax.random.dirichlet(jax.random.fold_in(_rk, 511), 0.3 * jnp.ones((16,), jnp.float32), (8, 128))
        _ctx_768t = jnp.einsum('bsk,bkd->bsd', _ctx_768c, _ctx_768P)
        _ctx_768t = _ctx_768t * jax.lax.rsqrt(jnp.mean(jnp.square(_ctx_768t)) + 1e-12) * 0.953939
        ctx_768 = -0.000191848 + 0.999787 * (_ctx_768t + 0.3 * jax.random.normal(jax.random.fold_in(_rk, 611), (8, 128, 96), jnp.float32))
        return (x, ctx_768)
    x, ctx_768 = _rec_inputs()

    def _L0_xattn_setup():
        import jax, jax.numpy as jnp
        import numpy as np
        N_HEADS = 16
        key = jax.random.key(seed)
        ks = jax.random.split(key, 8)
        b, l, m = (8, 128, 128)
        d_embed, d_cross = (128, 96)
        s_q = 1.0 / np.sqrt(d_embed)
        s_kv = 1.0 / np.sqrt(d_cross)
        return {'x': jax.random.normal(ks[0], (b, l, d_embed), jnp.float32), 'y': jax.random.normal(ks[1], (b, m, d_cross), jnp.float32), 'Wq': jax.random.normal(ks[2], (d_embed, d_embed), jnp.float32) * s_q, 'bq': jax.random.normal(ks[3], (d_embed,), jnp.float32) * 0.01, 'Wkv': jax.random.normal(ks[4], (2 * d_embed, d_cross), jnp.float32) * s_kv, 'bkv': jax.random.normal(ks[5], (2 * d_embed,), jnp.float32) * 0.01, 'Wo': jax.random.normal(ks[6], (d_embed, d_embed), jnp.float32) * s_q, 'bo': jax.random.normal(ks[7], (d_embed,), jnp.float32) * 0.01}
    _L0_xattn_all = _L0_xattn_setup()
    _L0_xattn_in = {k: v for k, v in _L0_xattn_all.items() if k in ('Wq', 'bq', 'Wkv', 'bkv', 'Wo', 'bo')}
    del _L0_xattn_all

    def _L0_ffn_setup():
        import jax, jax.numpy as jnp
        import numpy as np
        B, T, D, E = (4, 128, 128, 8)
        HD = 4 * D
        key = jax.random.key(seed)
        k1, k2, k3, k4 = jax.random.split(key, 4)
        std = 0.5 * D ** (-0.5)
        bound = 3.0 ** 0.5 * std
        x = jax.random.normal(k1, (B, T, D), dtype=jnp.float32)
        router_w = jax.random.normal(k2, (E, D), dtype=jnp.float32) * 0.02
        expert_fc = jax.random.uniform(k3, (E, D, HD), dtype=jnp.float32, minval=-bound, maxval=bound)
        expert_proj = jax.random.normal(k4, (E, D, HD), dtype=jnp.float32) * 0.02
        return {'x': x, 'router_w': router_w, 'expert_fc': expert_fc, 'expert_proj': expert_proj}
    _L0_ffn_all = _L0_ffn_setup()
    _L0_ffn_in = {k: v for k, v in _L0_ffn_all.items() if k in ('router_w', 'expert_fc', 'expert_proj')}
    del _L0_ffn_all

    def _L1_xattn_setup():
        import jax, jax.numpy as jnp
        import numpy as np
        NUM_HEADS = 16
        CLAMP = 10000.0
        key = jax.random.key(seed)
        ks = jax.random.split(key, 8)
        B, Nq, Nkv, Cq, Ckv = (4, 256, 256, 128, 96)
        s_q = 1.0 / np.sqrt(Cq)
        s_kv = 1.0 / np.sqrt(Ckv)
        return {'query': jax.random.normal(ks[0], (B, Nq, Cq), jnp.float32), 'key_value': jax.random.normal(ks[1], (B, Nkv, Ckv), jnp.float32), 'Wq': jax.random.normal(ks[2], (Cq, Cq), jnp.float32) * s_q, 'bq': jnp.zeros((Cq,), jnp.float32), 'Wk': jax.random.normal(ks[3], (Ckv, Cq), jnp.float32) * s_kv, 'bk': jnp.zeros((Cq,), jnp.float32), 'Wv': jax.random.normal(ks[4], (Ckv, Cq), jnp.float32) * s_kv, 'bv': jnp.zeros((Cq,), jnp.float32), 'Wo': jax.random.normal(ks[5], (Cq, Cq), jnp.float32) * s_q, 'bo': jnp.zeros((Cq,), jnp.float32)}
    _L1_xattn_all = _L1_xattn_setup()
    _L1_xattn_in = {k: v for k, v in _L1_xattn_all.items() if k in ('Wq', 'bq', 'Wk', 'bk', 'Wv', 'bv', 'Wo', 'bo')}
    del _L1_xattn_all

    def _L1_ffn_setup():
        import jax, jax.numpy as jnp
        import numpy as np
        B, S, D, H, E, K = (4, 256, 128, 256, 8, 2)
        TEMP = 5.0
        EPS = 1e-09
        key = jax.random.key(seed)
        k_x, k_wg, k_w1, k_w2 = jax.random.split(key, 4)
        scale = 0.02
        return {'x': jax.random.normal(k_x, (B, S, D), dtype=jnp.float32), 'Wg': jax.random.normal(k_wg, (D, E), dtype=jnp.float32) * scale, 'bg': jnp.zeros((E,), dtype=jnp.float32), 'W1': jax.random.normal(k_w1, (E, D, H), dtype=jnp.float32) * scale, 'b1': jnp.zeros((E, H), dtype=jnp.float32), 'W2': jax.random.normal(k_w2, (E, H, D), dtype=jnp.float32) * scale, 'b2': jnp.zeros((E, D), dtype=jnp.float32)}
    _L1_ffn_all = _L1_ffn_setup()
    _L1_ffn_in = {k: v for k, v in _L1_ffn_all.items() if k in ('Wg', 'bg', 'W1', 'b1', 'W2', 'b2')}
    del _L1_ffn_all
    return {'x': x, 'ctx_768': ctx_768, 'L0_xattn_Wq': _L0_xattn_in['Wq'], 'L0_xattn_bq': _L0_xattn_in['bq'], 'L0_xattn_Wkv': _L0_xattn_in['Wkv'], 'L0_xattn_bkv': _L0_xattn_in['bkv'], 'L0_xattn_Wo': _L0_xattn_in['Wo'], 'L0_xattn_bo': _L0_xattn_in['bo'], 'L0_ffn_router_w': _L0_ffn_in['router_w'], 'L0_ffn_expert_fc': _L0_ffn_in['expert_fc'], 'L0_ffn_expert_proj': _L0_ffn_in['expert_proj'], 'L1_xattn_Wq': _L1_xattn_in['Wq'], 'L1_xattn_bq': _L1_xattn_in['bq'], 'L1_xattn_Wk': _L1_xattn_in['Wk'], 'L1_xattn_bk': _L1_xattn_in['bk'], 'L1_xattn_Wv': _L1_xattn_in['Wv'], 'L1_xattn_bv': _L1_xattn_in['bv'], 'L1_xattn_Wo': _L1_xattn_in['Wo'], 'L1_xattn_bo': _L1_xattn_in['bo'], 'L1_ffn_Wg': _L1_ffn_in['Wg'], 'L1_ffn_bg': _L1_ffn_in['bg'], 'L1_ffn_W1': _L1_ffn_in['W1'], 'L1_ffn_b1': _L1_ffn_in['b1'], 'L1_ffn_W2': _L1_ffn_in['W2'], 'L1_ffn_b2': _L1_ffn_in['b2']}

def reference(x, ctx_768, L0_xattn_Wq, L0_xattn_bq, L0_xattn_Wkv, L0_xattn_bkv, L0_xattn_Wo, L0_xattn_bo, L0_ffn_router_w, L0_ffn_expert_fc, L0_ffn_expert_proj, L1_xattn_Wq, L1_xattn_bq, L1_xattn_Wk, L1_xattn_bk, L1_xattn_Wv, L1_xattn_bv, L1_xattn_Wo, L1_xattn_bo, L1_ffn_Wg, L1_ffn_bg, L1_ffn_W1, L1_ffn_b1, L1_ffn_W2, L1_ffn_b2):
    import jax
    import jax.numpy as jnp

    def _L0_xattn_ref(x, y, Wq, bq, Wkv, bkv, Wo, bo):
        import jax, jax.numpy as jnp
        import numpy as np
        N_HEADS = 16
        b, l, d = x.shape
        m = y.shape[1]
        h = N_HEADS
        dh = d // h
        q = (jnp.einsum('bld,ed->ble', x, Wq) + bq).reshape(b, l, h, dh)
        kv = (jnp.einsum('bmc,ec->bme', y, Wkv) + bkv).reshape(b, m, h, 2 * dh)
        k, v = (kv[..., :dh], kv[..., dh:])
        scale = 1.0 / jnp.sqrt(jnp.asarray(dh, x.dtype))
        att = jax.nn.softmax(jnp.einsum('blhd,bmhd->blmh', q, k) * scale, axis=2)
        out = jnp.einsum('blmh,bmhd->blhd', att, v).reshape(b, l, d)
        return jnp.einsum('bld,ed->ble', out, Wo) + bo

    def _L0_ffn_ref(x, router_w, expert_fc, expert_proj):
        import jax, jax.numpy as jnp
        import numpy as np
        B, T, D, E = (4, 128, 128, 8)
        HD = 4 * D
        logits = jnp.einsum('btd,ed->bte', x, router_w)
        probs = jax.nn.softmax(logits, axis=-1)
        expert_ids = jnp.argmax(probs, axis=-1)
        mask = jax.nn.one_hot(expert_ids, E, dtype=x.dtype)
        h = jnp.einsum('btd,edh->ebth', x, expert_fc)
        h = jnp.square(jax.nn.relu(h))
        out_e = jnp.einsum('ebth,edh->ebtd', h, expert_proj)
        output = jnp.einsum('ebtd,bte->btd', out_e, mask)
        return output

    def _L1_xattn_ref(query, key_value, Wq, bq, Wk, bk, Wv, bv, Wo, bo):
        import jax, jax.numpy as jnp
        import numpy as np
        NUM_HEADS = 16
        CLAMP = 10000.0
        B, Nq, Cq = query.shape
        Nkv = key_value.shape[1]
        H = NUM_HEADS
        D = Cq // H
        scale = D ** (-0.5)
        q = (query @ Wq + bq).reshape(B, Nq, H, D).transpose(0, 2, 1, 3)
        k = (key_value @ Wk + bk).reshape(B, Nkv, H, D).transpose(0, 2, 1, 3)
        v = (key_value @ Wv + bv).reshape(B, Nkv, H, D).transpose(0, 2, 1, 3)
        attn = jnp.einsum('bhqd,bhkd->bhqk', q, k) * scale
        attn = jnp.clip(attn, -CLAMP, CLAMP)
        attn = jax.nn.softmax(attn, axis=-1)
        attn = jnp.where(jnp.any(jnp.isnan(attn)), jnp.asarray(1.0 / Nkv, attn.dtype), attn)
        x = jnp.einsum('bhqk,bhkd->bqhd', attn, v).reshape(B, Nq, Cq)
        return x @ Wo + bo

    def _L1_ffn_ref(x, Wg, bg, W1, b1, W2, b2):
        import jax, jax.numpy as jnp
        import numpy as np
        B, S, D, H, E, K = (4, 256, 128, 256, 8, 2)
        TEMP = 5.0
        EPS = 1e-09
        logits = jnp.einsum('bsd,de->bse', x, Wg) + bg
        probs = jax.nn.softmax(logits / TEMP, axis=-1)
        vals, idx = jax.lax.top_k(probs, K)
        onehot = jax.nn.one_hot(idx, E, dtype=x.dtype)
        mask = jnp.einsum('bske,bsk->bse', onehot, vals)
        gates = mask / (jnp.sum(mask, axis=-1, keepdims=True) + EPS)
        h = jax.nn.gelu(jnp.einsum('bsd,edh->besh', x, W1) + b1[None, :, None, :], approximate=False)
        out = jnp.einsum('besh,ehd->besd', h, W2) + b2[None, :, None, :]
        y = jnp.einsum('bse,besd->bsd', gates, out)
        return y
    x = x + _L0_xattn_ref(_layernorm(x, axis=-1), ctx_768, L0_xattn_Wq, L0_xattn_bq, L0_xattn_Wkv, L0_xattn_bkv, L0_xattn_Wo, L0_xattn_bo)
    x = x + _L0_ffn_ref(_layernorm(x, axis=-1), L0_ffn_router_w, L0_ffn_expert_fc, L0_ffn_expert_proj)
    x = x + _L1_xattn_ref(_layernorm(x, axis=-1), ctx_768, L1_xattn_Wq, L1_xattn_bq, L1_xattn_Wk, L1_xattn_bk, L1_xattn_Wv, L1_xattn_bv, L1_xattn_Wo, L1_xattn_bo)
    x = x + _L1_ffn_ref(_layernorm(x, axis=-1), L1_ffn_Wg, L1_ffn_bg, L1_ffn_W1, L1_ffn_b1, L1_ffn_W2, L1_ffn_b2)
    return x

_drawn_inputs = setup_inputs


def setup_inputs(seed=0):
    import zlib

    import numpy as np

    out = dict(_drawn_inputs(seed))
    spreads = {'L1_xattn_bq': (0.0, 0.427),
     'L1_xattn_bk': (0.0, 0.8),
     'L1_xattn_bv': (0.0, 0.1),
     'L1_xattn_bo': (0.0, 0.1),
     'L1_ffn_bg': (0.0, 0.1),
     'L1_ffn_b1': (0.0, 0.8),
     'L1_ffn_b2': (0.0, 0.1)}
    factors = {'L0_xattn_bq': 8.0, 'L0_xattn_bkv': 4.019, 'L0_xattn_bo': 3.716, 'L1_ffn_W1': 2.726}
    for name, (base, spread) in spreads.items():
        noise = np.random.default_rng([zlib.crc32(name.encode()), seed]).standard_normal(out[name].shape)
        drawn = base * np.exp(spread * noise) if base else spread * noise
        out[name] = jnp.asarray(drawn.astype(out[name].dtype))
    for name, factor in factors.items():
        out[name] = (out[name] * factor).astype(out[name].dtype)
    return out
```

```python
import concourse.bass as bass
from concourse import mybir
from contextlib import ExitStack

B, L, D = 8, 128, 128
M, DC = 128, 96
H, DH = 16, 8
E = 8
F0, F1 = 4 * D, 2 * D
N = B * L
P = 128
C0, C1 = F0 // P, F1 // P
TILES = (N + E * (P - 1)) // P
XS_PARTS = [(0, 2), (2, 8), (8, TILES)]
SCALE = float(DH) ** -0.5
CLAMP = 10000.0 / SCALE
TEMP = 5.0
GATE_EPS = 1e-9
LN_EPS = 1e-5

A_COLS = dict(wk=128, wv=128, wq=128, bq=1, bk=1, bv=1)
R_COLS = dict(wo0=128, bo0=128, rw=8, wk=128, wv=128, wq=128, bq=1, bk=1, bv=1, wo1=128, bo1=128, wg=8, bg=8)


def columns(sizes):
    at, out = 0, {}
    for name, n in sizes.items():
        out[name] = (at, at + n)
        at += n
    return out, at


A_AT, A_N = columns(A_COLS)
R_AT, R_N = columns(R_COLS)


def build(nc, x_in, ctx_in, wa_in, wr_in, fc_in, proj_in, w1_in, w2_in, b2_in, out):
    fp32, bf16, i32 = mybir.dt.float32, mybir.dt.bfloat16, mybir.dt.int32
    ALU, ACT, AX = mybir.AluOpType, mybir.ActivationFunctionType, mybir.AxisListType.X

    slots_x = nc.dram_tensor("slots_x", (TILES * P, D), fp32, kind="Internal").ap()
    slots_y = nc.dram_tensor("slots_y", (TILES * P, D), fp32, kind="Internal").ap()

    ctx = ExitStack()
    with ctx:
        def sb(name, shape, dt=fp32):
            return ctx.enter_context(nc.sbuf_tensor(name, shape, dt))

        def sem(name):
            return ctx.enter_context(nc.semaphore(name))

        ident = sb("ident", [P, P])
        ones_bf = sb("ones_bf", [P, P], bf16)
        ones = sb("ones", [P, P])
        before = sb("before", [P, P], bf16)
        head_rows = sb("head_rows", [P, H])
        zeros = sb("zeros", [P, D])
        minus_half = sb("minus_half", [P, B])
        rank_down = sb("rank_down", [P, E])
        upto = sb("upto", [P, E, E])
        tile_no = sb("tile_no", [P, TILES])

        wa = sb("wa", [P, A_N])
        wr = sb("wr", [P, R_N])
        ctxT = sb("ctxT", [DC, B * M])
        fc = sb("fc", [P, E, F0])
        proj = sb("proj", [P, E, C0, D])
        w1 = sb("w1", [P, 2, F1 + C1])
        w2 = sb("w2", [P, 2, C1, D])
        b2 = sb("b2", [E, D])

        def wcol(layer, name):
            if layer == 0 and name in A_AT:
                lo, hi = A_AT[name]
                return wa[:, lo:hi]
            lo, hi = R_AT[name + str(layer) if name in ("wo", "bo") else name]
            return wr[:, lo:hi]

        xr = sb("xr", [P, B, D])
        xn = sb("xn", [P, B, D])
        xT = sb("xT", [P, N])
        qT = sb("qT", [P, N])
        kT = sb("kT", [P, N])
        kmask = sb("kmask", [P, B, H, M])
        vaug = [sb(f"vaug{i}", [P, B, H, 32]) for i in range(2)]
        work = sb("work", [P, 4096])
        work2 = sb("work2", [P, 2048])
        S_sb = work[:].rearrange("p (b u n) -> p b u n", b=2, u=2)
        mx = sb("mx", [P, B, H])
        PT = work2[:].rearrange("p (k n) -> p k n", k=4)
        osb = sb("osb", [P, 2, 256])
        rc = sb("rc", [P, 2, H])
        att = sb("att", [P, 2, D])
        OT = sb("OT", [P, B, L])
        stats = sb("stats", [P, B, 6])
        mv = sb("mv", [P, B, 2])
        ve = sb("ve", [P, B])
        rstd = sb("rstd", [P, B])
        ksum = sb("ksum", [P, B])
        ctxsum = sb("ctxsum", [DC, B])
        vmean = sb("vmean", [P, B])
        tn = sb("tn", [P, B])
        tn2 = sb("tn2", [P, B])
        nan_rows = sb("nan_rows", [P, 1])
        nan_any = sb("nan_any", [P, 1], i32)
        lg = sb("lg", [P, B, E])
        lgm = sb("lgm", [P, B])
        eq = sb("eq", [P, B, E])
        oh = sb("oh", [P, B, E], bf16)
        oh2 = sb("oh2", [P, B, E])
        tiles_i = sb("tiles_i", [P, E], i32)
        tiles_f = sb("tiles_f", [P, E])
        upsel = sb("upsel", [P, E, E])
        ends = sb("ends", [P, E])
        base = sb("base", [P, E])
        slot_f = sb("slot_f", [P, B])
        slot_i = sb("slot_i", [P, B], i32)
        cmp = sb("cmp", [P, TILES, E])
        eid_f = sb("eid_f", [P, TILES])
        eid = sb("eid", [P, TILES], i32)
        xs = work[:, 0:TILES * D].rearrange("p (t d) -> p t d", d=D)
        xsT = sb("xsT", [P, 2, P])
        fcb = work[:, 2048:3072].rearrange("p (t f) -> p t f", t=2)
        hr = work[:, 3072:4096].rearrange("p (t f) -> p t f", t=2)
        h2 = work2[:, 0:1024].rearrange("p (t f) -> p t f", t=2)
        ys = sb("ys", [P, 2, D])
        yg = work2[:, 1024:2048].rearrange("p (b d) -> p b d", d=D)
        pr = sb("pr", [P, B, E])
        p2 = sb("p2", [P, B, E])
        m1 = sb("m1", [P, B])
        m2 = sb("m2", [P, B])
        gsum = sb("gsum", [P, B])
        gates = sb("gates", [P, B, E])
        gT = sb("gT", [E, B, L])
        hT = work2[:].rearrange("p (h c n) -> p h c n", h=2, c=C1)

        ps = ctx.enter_context(nc.psum_tensor("ps", [P, 8, 512], fp32))

        s_x, s_ctx, s_wa, s_wr = sem("s_x"), sem("s_ctx"), sem("s_wa"), sem("s_wr")
        s_fc, s_b2, s_zero = sem("s_fc"), sem("s_b2"), sem("s_zero")
        s_w12 = [sem("s_w12_0"), sem("s_w12_1")]
        pool_const = sem("pool_const")
        dve_const = sem("dve_const")
        dve_chain, act_chain, pool_chain = sem("dve_chain"), sem("act_chain"), sem("pool_chain")
        ln_var, ln_rstd, ln_norm, ln_tr, ln_xT = (sem(n) for n in ("ln_var", "ln_rstd", "ln_norm", "ln_tr", "ln_xT"))
        bo_added = sem("bo_added")
        k_ps, k_sb, v_ps, v_sb, q_ps, q_sb = (sem(n) for n in ("k_ps", "k_sb", "v_ps", "v_sb", "q_ps", "q_sb"))
        kmask_dve, kmask_act, kmask_dma = sem("kmask_dve"), sem("kmask_act"), sem("kmask_dma")
        guard_in, guard_ps, guard_cnt, guard_tot, guard_rdy = (
            sem(n) for n in ("guard_in", "guard_ps", "guard_cnt", "guard_tot", "guard_rdy"))
        s_ps, s_sub, p_rdy, pt_ps, pt_sb, o_ps, o_sb, t_ps, att_sb, a_ps, ot_sb, y_ps, x_attn = (
            sem(n) for n in ("s_ps", "s_sub", "p_rdy", "pt_ps", "pt_sb", "o_ps", "o_sb", "t_ps", "att_sb",
                             "a_ps", "ot_sb", "y_ps", "x_attn"))
        lg_ps, oh_rdy, cum_ps, slot_rdy, eid_rdy = (
            sem(n) for n in ("lg_ps", "oh_rdy", "cum_ps", "slot_rdy", "eid_rdy"))
        scattered, xsT_ps, xsT_sb, fc_rdy, h_ps, h_relu, h_sq, yt_ps, yt_sb = (
            sem(n) for n in ("scattered", "xsT_ps", "xsT_sb", "fc_rdy", "h_ps", "h_relu", "h_sq", "yt_ps", "yt_sb"))
        lg1_ps, lg1_sub, lg1_exp, gates_rdy, gT_ps, gT_sb, b2_ps, b2_added = (
            sem(n) for n in ("lg1_ps", "lg1_sub", "lg1_exp", "gates_rdy", "gT_ps", "gT_sb", "b2_ps", "b2_added"))
        up_ps, hT_rdy, dn_ps, x_exp = (sem(n) for n in ("up_ps", "hT_rdy", "dn_ps", "x_exp"))
        s_out = sem("s_out")

        xs_in = [sem(f"xs_in{i}") for i in range(len(XS_PARTS))]
        y_out = [sem(f"y_out{i}") for i in range(2)]
        gathered = [sem(f"gathered{b}") for b in range(B)]

        CONSTS = 7
        BU = lambda l, b, u: (l * B + b) * 2 + u + 1
        BK = lambda l, b, k: (l * B + b) * 4 + k + 1
        BB = lambda l, b: l * B + b + 1

        block = ctx.enter_context(nc.Block())

        @block.sync
        def _(sp):
            sp.dma_start(ctxT[:], ctx_in).then_inc(s_ctx, 16)
            sp.dma_start(wa[:], wa_in).then_inc(s_wa, 16)
            sp.dma_start(wr[:], wr_in).then_inc(s_wr, 16)
            sp.dma_start(fc[:], fc_in).then_inc(s_fc, 16)
            sp.dma_start(proj[:], proj_in).then_inc(s_fc, 16)
            sp.dma_start(b2[:], b2_in).then_inc(s_b2, 16)
            sp.dma_start(w1[:, 0, :], w1_in[0]).then_inc(s_w12[0], 16)
            sp.dma_start(w2[:, 0], w2_in[0]).then_inc(s_w12[0], 16)
            sp.dma_start(w1[:, 1, :], w1_in[1]).then_inc(s_w12[1], 16)
            sp.dma_start(w2[:, 1], w2_in[1]).then_inc(s_w12[1], 16)
            sp.wait_ge(pool_const, CONSTS)
            sp.dma_start(slots_x.rearrange("(t p) d -> p t d", p=P),
                         zeros[:].unsqueeze(1).to_broadcast([P, TILES, D])).then_inc(s_zero, 16)

            sp.wait_ge(k_sb, 4)
            sp.wait_ge(s_ps, BU(0, B - 1, 1))
            for h in range(H):
                sp.dma_start(kmask[DH * h:DH * (h + 1), :, h, :],
                             kT[DH * h:DH * (h + 1), :].rearrange("p (b m) -> p b m", b=B)).then_inc(kmask_dma, 16)

            sp.wait_ge(scattered, 16 * B)
            for i, (lo, hi) in enumerate(XS_PARTS):
                sp.dma_start(xs[:, lo:hi, :], slots_x.rearrange("(t p) d -> p t d", p=P)[:, lo:hi, :]).then_inc(xs_in[i], 16)
            for t in range(TILES):
                sp.wait_ge(yt_sb, t + 1)
                sp.dma_start(slots_y[t * P:(t + 1) * P, :], ys[:, t % 2, :]).then_inc(y_out[t % 2], 16)

            for e in range(2, E):
                sp.wait_ge(dn_ps, 2 * (e - 1))
                sp.dma_start(w1[:, e % 2, :], w1_in[e]).then_inc(s_w12[e % 2], 16)
                sp.dma_start(w2[:, e % 2], w2_in[e]).then_inc(s_w12[e % 2], 16)
            for half in range(2):
                sp.wait_ge(x_exp, 2 * (E - 1) + half + 1)
                sp.dma_start(out.rearrange("(b t) d -> t b d", t=L)[:, 4 * half:4 * half + 4, :],
                             xr[:, 4 * half:4 * half + 4, :]).then_inc(s_out, 16)
            sp.wait_ge(s_out, 32)

        @block.gpsimd
        def _(pool):
            count = [0]

            def link(ins):
                count[0] += 1
                ins.then_inc(pool_chain, 1)
                pool.wait_ge(pool_chain, count[0])

            link(nc.gpsimd.memset(ones[:], 1.0))
            nc.gpsimd.affine_select(out=ident[:], in_=ones[:], pattern=[[-1, P]], compare_op=ALU.is_equal,
                                    fill=0.0, base=0, channel_multiplier=1).then_inc(pool_const, 1)
            link(nc.gpsimd.memset(head_rows[:], 1.0))
            link(nc.gpsimd.affine_select(out=head_rows[:], in_=head_rows[:], pattern=[[-DH, H]],
                                         compare_op=ALU.is_ge, fill=0.0, base=0, channel_multiplier=1))
            nc.gpsimd.affine_select(out=head_rows[:], in_=head_rows[:], pattern=[[DH, H]],
                                    compare_op=ALU.is_gt, fill=0.0, base=DH, channel_multiplier=-1).then_inc(pool_const, 1)
            nc.gpsimd.memset(minus_half[:], -0.5).then_inc(pool_const, 1)
            nc.gpsimd.memset(zeros[:], 0.0).then_inc(pool_const, 1)
            nc.gpsimd.iota(rank_down[:], pattern=[[-1, E]], base=E, channel_multiplier=0,
                           allow_small_or_imprecise_dtypes=True).then_inc(pool_const, 1)
            nc.gpsimd.iota(tile_no[:], pattern=[[1, TILES]], base=0, channel_multiplier=0,
                           allow_small_or_imprecise_dtypes=True).then_inc(pool_const, 1)
            link(nc.gpsimd.memset(upto[:], 1.0))
            nc.gpsimd.affine_select(out=upto[:], in_=upto[:], pattern=[[1, E], [-1, E]], compare_op=ALU.is_ge,
                                    fill=0.0, base=0, channel_multiplier=0).then_inc(pool_const, 1)
            link(nc.gpsimd.memset(ones_bf[:], 1.0))
            link(nc.gpsimd.affine_select(out=before[:], in_=ones_bf[:], pattern=[[1, P]], compare_op=ALU.is_gt,
                                         fill=0.0, base=0, channel_multiplier=-1))

            def rsqrt(k, half):
                pool.wait_ge(ln_var, 2 * k + half + 1)
                sl = slice(4 * half, 4 * half + 4)
                nc.gpsimd.tensor_tensor(rstd[:, sl], ve[:, sl], minus_half[:, sl], ALU.pow).then_inc(ln_rstd, 1)

            def add_bo(layer, k):
                pool.wait_ge(s_wr, 16)
                for half in range(2):
                    pool.wait_ge(ln_norm, 2 * k + half + 1)
                    sl = slice(4 * half, 4 * half + 4)
                    nc.gpsimd.tensor_tensor(xr[:, sl, :], xr[:, sl, :],
                                            wcol(layer, "bo").unsqueeze(1).to_broadcast([P, 4, D]),
                                            ALU.add).then_inc(bo_added, 1)

            rsqrt(0, 0)
            rsqrt(0, 1)
            add_bo(0, 0)
            rsqrt(1, 0)
            rsqrt(1, 1)
            pool.wait_ge(slot_rdy, 1)
            pool.wait_ge(s_zero, 16)
            pool.wait_ge(ln_norm, 4)
            for b in range(B):
                pool.indirect_dma_start(slots_x, bass.IndirectOffsetOnAxis(slot_i[:, b:b + 1], 0),
                                        xn[:, b, :], None).then_inc(scattered, 16)
            pool.wait_ge(y_out[0], 16 * ((TILES + 1) // 2))
            pool.wait_ge(y_out[1], 16 * (TILES // 2))
            for b in range(B):
                pool.indirect_dma_start(yg[:, b, :], None, slots_y,
                                        bass.IndirectOffsetOnAxis(slot_i[:, b:b + 1], 0)).then_inc(gathered[b], 16)
                if b == 5:
                    rsqrt(2, 0)
            rsqrt(2, 1)
            add_bo(1, 2)
            rsqrt(3, 0)
            rsqrt(3, 1)

        @block.scalar
        def _(act):
            act.dma_start(xr[:], x_in.rearrange("(b t) d -> t b d", t=L)).then_inc(s_x, 16)
            count = [0]

            def link(ins):
                count[0] += 1
                ins.then_inc(act_chain, 1)
                act.wait_ge(act_chain, count[0])

            def ln_evac(k):
                for half in range(2):
                    act.wait_ge(ln_tr, 2 * k + half + 1)
                    if k == 1 and half == 0:
                        act.wait_ge(q_ps, 2)
                    if k == 2 and half == 0:
                        act.wait_ge(lg_ps, 1)
                    if k == 3 and half == 0:
                        act.wait_ge(q_ps, 4)
                    nc.scalar.activation(xT[:, 512 * half:512 * half + 512], ps[:, 4 + half, :], ACT.Copy).then_inc(ln_xT, 1)

            def k_evac(layer, bank):
                act.wait_ge(s_wa if layer == 0 else s_wr, 16)
                if layer == 1:
                    act.wait_ge(kmask_dve, 2)
                    act.wait_ge(kmask_act, 2)
                for half in range(2):
                    act.wait_ge(k_ps, 2 * layer + half + 1)
                    nc.scalar.activation(kT[:, 512 * half:512 * half + 512], ps[:, bank + half, :], ACT.Identity,
                                         bias=wcol(layer, "bk")).then_inc(k_sb, 1)

            def q_evac(layer):
                for half in range(2):
                    act.wait_ge(q_ps, 2 * layer + half + 1)
                    nc.scalar.activation(qT[:, 512 * half:512 * half + 512], ps[:, 6 + half, :], ACT.Identity,
                                         bias=wcol(layer, "bq")).then_inc(q_sb, 1)

            def attention(layer):
                def exp(b):
                    for u in range(2):
                        act.wait_ge(s_sub, BU(layer, b, u))
                        z = S_sb[:, b % 2, u, :]
                        if layer == 0:
                            nc.scalar.activation(z, z, ACT.Exp, scale=SCALE).then_inc(p_rdy, 1)
                        else:
                            link(nc.scalar.activation(z, z, ACT.Relu, scale=-1.0))
                            nc.scalar.activation(z, z, ACT.Exp, scale=-SCALE).then_inc(p_rdy, 1)

                def pt_evac(b, k):
                    act.wait_ge(pt_ps, BK(layer, b, k))
                    if layer + b > 0:
                        act.wait_ge(o_ps, 4 * (layer * B + b - 1) + k + 1)
                    nc.scalar.activation(PT[:, k, :], ps[:, 4 + k % 2, :], ACT.Copy).then_inc(pt_sb, 1)

                def o_evac(b):
                    act.wait_ge(o_ps, 4 * (layer * B + b) + 4)
                    if layer * B + b >= 2:
                        act.wait_ge(t_ps, layer * B + b - 1)
                    nc.scalar.activation(osb[:, b % 2, :], ps[:, 6, 0:256], ACT.Copy).then_inc(o_sb, 1)

                exp(0)
                for b in range(B):
                    for k in range(4):
                        pt_evac(b, k)
                        if k == 1 and b + 1 < B:
                            exp(b + 1)
                        if k == 1 and b > 0 and False:
                            pass
                    o_evac(b)

            act.wait_ge(s_wa, 16)
            k_evac(0, 0)
            ln_evac(0)
            for half in range(2):
                act.wait_ge(k_sb, half + 1)
                if half == 0:
                    act.wait_ge(pool_const, CONSTS)
                for h in range(H // 2, H):
                    ins = nc.scalar.activation(kmask[:, 4 * half:4 * half + 4, h, :],
                                               kT[:, 512 * half:512 * half + 512].rearrange("p (b m) -> p b m", m=M),
                                               ACT.Copy, scale=head_rows[:, h:h + 1])
                ins.then_inc(kmask_act, 1)
                if half == 0:
                    q_evac(0)
            attention(0)

            ln_evac(1)
            def fc_copy(t):
                expert = act.value_load(eid[0:1, t:t + 1], min_val=0, max_val=E - 1)
                if t >= 2:
                    act.wait_ge(h_ps, t - 1)
                nc.scalar.activation(fcb[:, t % 2, :], fc[:, bass.ds(expert, 1), :].rearrange("p a f -> p (a f)"),
                                     ACT.Copy).then_inc(fc_rdy, 1)

            k_evac(1, 6)
            act.wait_ge(eid_rdy, 1)
            act.wait_ge(s_fc, 32)
            fc_copy(0)
            fc_copy(1)
            for t in range(TILES):
                act.wait_ge(h_ps, t + 1)
                if t >= 2:
                    act.wait_ge(h_sq, t - 1)
                nc.scalar.activation(hr[:, t % 2, :], ps[:, t % 2, :], ACT.Relu).then_inc(h_relu, 1)
                if t + 2 < TILES:
                    fc_copy(t + 2)

            ln_evac(2)
            q_evac(1)
            attention(1)
            ln_evac(3)
            act.wait_ge(lg1_sub, 1)
            nc.scalar.activation(pr[:], lg[:], ACT.Exp, scale=1.0 / TEMP).then_inc(lg1_exp, 1)
            act.wait_ge(gT_ps, 1)
            nc.scalar.activation(gT[:].rearrange("p b l -> p (b l)"), ps[0:E, 6:8, :].rearrange("p a n -> p (a n)"),
                                 ACT.Copy).then_inc(gT_sb, 1)
            for e in range(E):
                act.wait_ge(s_w12[e % 2], 32 * (e // 2 + 1))
                for half in range(2):
                    for c in range(C1):
                        act.wait_ge(up_ps, (2 * e + half) * C1 + c + 1)
                        if e > 0:
                            act.wait_ge(dn_ps, 2 * (e - 1) + half + 1)
                        nc.scalar.activation(hT[:, half, c, :], ps[:, 2 * half + c, :], ACT.Gelu,
                                             bias=w1[:, e % 2, F1 + c:F1 + c + 1]).then_inc(hT_rdy, 1)

        @block.vector
        def _(dve):
            count = [0]

            def link(ins):
                count[0] += 1
                ins.then_inc(dve_chain, 1)
                dve.wait_ge(dve_chain, count[0])

            def ln(k):
                for half in range(2):
                    bs = range(4 * half, 4 * half + 4)
                    sl = slice(4 * half, 4 * half + 4)
                    if k == 2:
                        for b in bs:
                            dve.wait_ge(gathered[b], 16)
                            ins = nc.vector.tensor_tensor(xr[:, b, :], xr[:, b, :], yg[:, b, :], ALU.add)
                        link(ins)
                    for b in bs:
                        ins = nc.vector.bn_stats(stats[:, b, :], xr[:, b, :])
                    link(ins)
                    for b in bs:
                        ins = nc.vector.bn_aggr(mv[:, b, :], stats[:, b, :])
                    link(ins)
                    nc.vector.tensor_scalar(ve[:, sl], mv[:, sl, 1], LN_EPS, None, ALU.add).then_inc(ln_var, 1)
                for half in range(2):
                    dve.wait_ge(ln_rstd, 2 * k + half + 1)
                    if k == 2 and half == 0:
                        dve.wait_ge(scattered, 16 * B)
                    if k in (1, 3) and half == 0:
                        dve.wait_ge(ln_tr, 2 * k)
                    for b in range(4 * half, 4 * half + 4):
                        ins = nc.vector.tensor_scalar(xn[:, b, :], xr[:, b, :], mv[:, b, 0:1], rstd[:, b:b + 1],
                                                      ALU.subtract, ALU.mult)
                    ins.then_inc(ln_norm, 1)

            def v_evac(layer, bank):
                dve.wait_ge(v_ps, layer + 1)
                src = ps[:, bank:bank + 2, :].rearrange("p k (q g x) -> p (k q) g x", g=4, x=16)
                dst = vaug[layer][:].rearrange("p b (c j g) x -> p (b c) j g x", c=2, j=2)
                for j in range(2):
                    ins = nc.vector.tensor_copy(dst[:, :, j, :, 8 * j:8 * j + 8], src[:, :, :, 8 * j:8 * j + 8])
                ins.then_inc(v_sb, 1)

            def attention(layer):
                def scores(b):
                    for u in range(2):
                        dve.wait_ge(s_ps, BU(layer, b, u))
                        s = ps[:, 2 * u:2 * u + 2, :].rearrange("p k (h m) -> p (k h) m", m=M)
                        top = mx[:, b, 8 * u:8 * u + 8]
                        link(nc.vector.tensor_reduce(top, s, axis=AX, op=ALU.max))
                        if layer == 1:
                            link(nc.vector.tensor_scalar(top, top, -CLAMP, CLAMP, ALU.max, ALU.min))
                        if b >= 2:
                            dve.wait_ge(pt_ps, BK(layer, b - 2, 2 * u + 1))
                        z = S_sb[:, b % 2, u, :].rearrange("p (h m) -> p h m", m=M)
                        topb = top.unsqueeze(2).to_broadcast([P, 8, M])
                        if layer == 0:
                            ins = nc.vector.tensor_tensor(z, s, topb, ALU.subtract)
                        else:
                            ins = nc.vector.scalar_tensor_tensor(z, s, -CLAMP, topb, ALU.max, ALU.subtract)
                        ins.then_inc(s_sub, 1)

                def norm(b):
                    dve.wait_ge(t_ps, BB(layer, b))
                    t = ps[:, 7, 0:256].rearrange("p (q x) -> p q x", x=32)
                    link(nc.vector.reciprocal(rc[:, b % 2, :].rearrange("p (q j) -> p q j", j=2), t[:, :, 16:18]))
                    if layer * B + b >= 2:
                        dve.wait_ge(a_ps, layer * B + b - 1)
                    nc.vector.tensor_tensor(
                        att[:, b % 2, :].rearrange("p (q j d) -> p q j d", j=2, d=DH),
                        t[:, :, 0:16].rearrange("p q (j d) -> p q j d", d=DH),
                        rc[:, b % 2, :].rearrange("p (q j) -> p q j", j=2).unsqueeze(3).to_broadcast([P, 8, 2, DH]),
                        ALU.mult).then_inc(att_sb, 1)

                def ot(b):
                    dve.wait_ge(a_ps, BB(layer, b))
                    ins = nc.vector.tensor_scalar(OT[:, b, :], ps[:, 7, 256:384], wcol(layer, "bv"), None, ALU.add)
                    if layer == 1:
                        link(ins)
                        ins = nc.vector.copy_predicated(OT[:, b, :], nan_any[:, 0:1].to_broadcast([P, L]),
                                                        vmean[:, b:b + 1].to_broadcast([P, L]))
                    ins.then_inc(ot_sb, 1)

                scores(0)
                if layer == 1:
                    guard()
                scores(1)
                for b in range(B):
                    if b + 2 < B:
                        scores(b + 2)
                    norm(b)
                    ot(b)
                for half in range(2):
                    dve.wait_ge(y_ps, 2 * layer + half + 1)
                    dve.wait_ge(bo_added, 2 * layer + half + 1)
                    sl = slice(4 * half, 4 * half + 4)
                    ins = nc.vector.tensor_tensor(xr[:, sl, :], ps[:, 4 + half, :].rearrange("p (b d) -> p b d", b=4),
                                                  xr[:, sl, :], ALU.add)
                link(ins)

            def guard():
                dve.wait_ge(guard_ps, 1)
                nc.vector.tensor_copy(tn[:], ps[:, 7, 0:B])
                link(nc.vector.tensor_scalar(vmean[:], ps[:, 7, B:2 * B], 1.0 / M, wcol(1, "bv"), ALU.mult, ALU.add))
                link(nc.vector.tensor_tensor(tn2[:], tn[:], tn[:], ALU.not_equal))
                nc.vector.tensor_reduce(nan_rows[:], tn2[:], axis=AX, op=ALU.add).then_inc(guard_cnt, 1)
                dve.wait_ge(guard_tot, 1)
                link(nc.vector.tensor_scalar(nan_any[:], ps[:, 7, 16:17], 0.5, None, ALU.is_gt))

            def first_max(src, top, onehot):
                link(nc.vector.tensor_reduce(top[:], src[:], axis=AX, op=ALU.max))
                link(nc.vector.tensor_tensor(eq[:], src[:], top[:].unsqueeze(2).to_broadcast([P, B, E]), ALU.is_equal))
                link(nc.vector.tensor_tensor(eq[:], eq[:], rank_down[:].unsqueeze(1).to_broadcast([P, B, E]), ALU.mult))
                link(nc.vector.tensor_reduce(lgm[:], eq[:], axis=AX, op=ALU.max))
                return nc.vector.tensor_tensor(onehot[:], eq[:], lgm[:].unsqueeze(2).to_broadcast([P, B, E]), ALU.is_equal)

            for i in range(2):
                link(nc.vector.memset(vaug[i][:], 0.0))
                va = vaug[i][:].rearrange("p b (c j g) x -> p (b c) j g x", c=2, j=2)
                for j in range(2):
                    nc.vector.memset(va[:, :, j, :, 16 + j:17 + j], 1.0)
            dve.wait_ge(s_x, 16)
            ln(0)
            for half in range(2):
                dve.wait_ge(k_sb, half + 1)
                if half == 0:
                    dve.wait_ge(pool_const, CONSTS)
                for h in range(H // 2):
                    ins = nc.vector.tensor_scalar(kmask[:, 4 * half:4 * half + 4, h, :],
                                                  kT[:, 512 * half:512 * half + 512].rearrange("p (b m) -> p b m", m=M),
                                                  head_rows[:, h:h + 1], None, ALU.mult)
                ins.then_inc(kmask_dve, 1)
                if half == 0:
                    v_evac(0, 2)
            dve.wait_ge(s_wa, 16)
            attention(0)

            ln(1)
            dve.wait_ge(lg_ps, 1)
            link(nc.vector.tensor_copy(lg[:], ps[:, 6, 0:64].rearrange("p (b e) -> p b e", e=E)))
            first_max(lg, m1, oh).then_inc(oh_rdy, 1)
            dve.wait_ge(cum_ps, 1)
            link(nc.vector.tensor_scalar(tiles_i[:], ps[:, 7, 64:72], float(P - 1), None, ALU.add))
            link(nc.vector.tensor_scalar(tiles_i[:], tiles_i[:], 7, None, ALU.logical_shift_right))
            link(nc.vector.tensor_copy(tiles_f[:], tiles_i[:]))
            link(nc.vector.tensor_tensor(upsel[:], upto[:], tiles_f[:].unsqueeze(1).to_broadcast([P, E, E]), ALU.mult))
            link(nc.vector.tensor_reduce(ends[:], upsel[:], axis=AX, op=ALU.add))
            link(nc.vector.tensor_tensor(base[:], ends[:], tiles_f[:], ALU.subtract))
            link(nc.vector.tensor_scalar(base[:], base[:], float(P), None, ALU.mult))
            link(nc.vector.tensor_tensor(oh2[:], ps[:, 7, 0:64].rearrange("p (b e) -> p b e", e=E),
                                         base[:].unsqueeze(1).to_broadcast([P, B, E]), ALU.add))
            link(nc.vector.tensor_tensor(oh2[:], oh2[:], oh[:], ALU.mult))
            link(nc.vector.tensor_reduce(slot_f[:], oh2[:], axis=AX, op=ALU.add))
            nc.vector.tensor_copy(slot_i[:], slot_f[:]).then_inc(slot_rdy, 1)
            link(nc.vector.tensor_tensor(cmp[:], ends[:].unsqueeze(1).to_broadcast([P, TILES, E]),
                                         tile_no[:].unsqueeze(2).to_broadcast([P, TILES, E]), ALU.is_le))
            link(nc.vector.tensor_reduce(eid_f[:], cmp[:], axis=AX, op=ALU.add))
            nc.vector.tensor_scalar(eid[:], eid_f[:], float(E - 1), None, ALU.min).then_inc(eid_rdy, 1)

            v_evac(1, 6)
            dve.wait_ge(k_sb, 4)
            nc.vector.tensor_reduce(ksum[:], kT[:].rearrange("p (b m) -> p b m", m=M), axis=AX, op=ALU.add)
            nc.vector.tensor_reduce(ctxsum[:], ctxT[:].rearrange("p (b m) -> p b m", m=M), axis=AX,
                                    op=ALU.add).then_inc(guard_in, 1)

            def xsT_evac(t):
                dve.wait_ge(xsT_ps, t + 1)
                if t >= 2:
                    dve.wait_ge(h_ps, t - 1)
                nc.vector.tensor_copy(xsT[:, t % 2, :], ps[:, 2, 0:P]).then_inc(xsT_sb, 1)

            def y_evac(t):
                dve.wait_ge(yt_ps, t + 1)
                if t >= 2:
                    dve.wait_ge(y_out[t % 2], 16 * (t // 2))
                nc.vector.tensor_copy(ys[:, t % 2, :], ps[:, 3, 0:D]).then_inc(yt_sb, 1)

            xsT_evac(0)
            for t in range(TILES):
                if t + 1 < TILES:
                    xsT_evac(t + 1)
                dve.wait_ge(h_relu, t + 1)
                if t >= 2:
                    dve.wait_ge(yt_ps, t - 1)
                nc.vector.tensor_tensor(h2[:, t % 2, :], hr[:, t % 2, :], hr[:, t % 2, :], ALU.mult).then_inc(h_sq, 1)
                if t >= 1:
                    y_evac(t - 1)
            y_evac(TILES - 1)

            ln(2)
            attention(1)
            ln(3)
            dve.wait_ge(lg1_ps, 1)
            link(nc.vector.tensor_tensor(lg[:], ps[:, 6, 0:64].rearrange("p (b e) -> p b e", e=E),
                                         wcol(1, "bg").unsqueeze(1).to_broadcast([P, B, E]), ALU.add))
            link(nc.vector.tensor_reduce(m1[:], lg[:], axis=AX, op=ALU.max))
            nc.vector.tensor_tensor(lg[:], lg[:], m1[:].unsqueeze(2).to_broadcast([P, B, E]), ALU.subtract).then_inc(lg1_sub, 1)
            dve.wait_ge(lg1_exp, 1)
            link(nc.vector.tensor_reduce(gsum[:], pr[:], axis=AX, op=ALU.add))
            link(nc.vector.reciprocal(gsum[:], gsum[:]))
            link(nc.vector.tensor_tensor(pr[:], pr[:], gsum[:].unsqueeze(2).to_broadcast([P, B, E]), ALU.mult))
            link(first_max(pr, m1, oh2))
            link(nc.vector.scalar_tensor_tensor(p2[:], oh2[:], -2.0, pr[:], ALU.mult, ALU.add))
            link(first_max(p2, m2, gates))
            link(nc.vector.tensor_tensor(gates[:], gates[:], oh2[:], ALU.add))
            link(nc.vector.tensor_tensor(gates[:], gates[:], pr[:], ALU.mult))
            link(nc.vector.tensor_tensor(gsum[:], m1[:], m2[:], ALU.add))
            link(nc.vector.tensor_scalar(gsum[:], gsum[:], GATE_EPS, None, ALU.add))
            link(nc.vector.reciprocal(gsum[:], gsum[:]))
            ins = nc.vector.tensor_tensor(gates[:], gates[:], gsum[:].unsqueeze(2).to_broadcast([P, B, E]), ALU.mult)
            ins.then_inc(gates_rdy, 1)
            dve.wait_ge(gates_rdy, 1)
            dve.wait_ge(b2_ps, 1)
            ins = nc.vector.tensor_tensor(xr[:].rearrange("p b d -> p (b d)"), ps[:, 6:8, :].rearrange("p a n -> p (a n)"),
                                          xr[:].rearrange("p b d -> p (b d)"), ALU.add)
            link(ins)
            for e in range(E):
                for half in range(2):
                    dve.wait_ge(dn_ps, 2 * e + half + 1)
                    if e > 0:
                        dve.wait_ge(x_exp, 2 * (e - 1) + half + 1)
                    for i in range(4):
                        b = 4 * half + i
                        ins = nc.vector.scalar_tensor_tensor(xr[:, b, :], ps[:, 4 + half, 128 * i:128 * i + 128],
                                                             gates[:, b, e:e + 1], xr[:, b, :], ALU.mult, ALU.add)
                    ins.then_inc(x_exp, 1)

        @block.tensor
        def _(pe):
            mm = nc.tensor.matmul

            def k_proj(layer, bank):
                for half in range(2):
                    mm(ps[:, bank + half, :], wcol(layer, "wk")[0:DC, :], ctxT[:, 512 * half:512 * half + 512],
                       start=True, stop=True).then_inc(k_ps, 1)

            def v_proj(layer, bank):
                for b in range(B):
                    ins = mm(ps[:, bank + b // 4, 128 * (b % 4):128 * (b % 4) + 128], ctxT[:, M * b:M * b + M],
                             wcol(layer, "wv")[0:DC, :], start=True, stop=True)
                ins.then_inc(v_ps, 1)

            def ln_transpose(k):
                for half in range(2):
                    pe.wait_ge(ln_norm, 2 * k + half + 1)
                    for i in range(4):
                        ins = nc.tensor.transpose(ps[:, 4 + half, 128 * i:128 * i + 128], xn[:, 4 * half + i, :], ident[:])
                    ins.then_inc(ln_tr, 1)

            def q_proj(layer):
                for half in range(2):
                    pe.wait_ge(ln_xT, 4 * layer + half + 1)
                    mm(ps[:, 6 + half, :], wcol(layer, "wq"), xT[:, 512 * half:512 * half + 512],
                       start=True, stop=True).then_inc(q_ps, 1)

            def attention(layer):
                def scores(b, u):
                    if b % 4 == 0 and u == 0:
                        pe.wait_ge(q_sb, 2 * layer + b // 4 + 1)
                        if layer == 0:
                            pe.wait_ge(kmask_dve, b // 4 + 1)
                            pe.wait_ge(kmask_act, b // 4 + 1)
                    if b > 0:
                        pe.wait_ge(s_sub, BU(layer, b - 1, u))
                    for i in range(2):
                        h = 8 * u + 4 * i
                        ins = mm(ps[:, 2 * u + i, :], qT[:, L * b:L * b + L],
                                 kmask[:, b, h:h + 4, :].rearrange("p h m -> p (h m)"), start=True, stop=True)
                    ins.then_inc(s_ps, 1)

                def p_transpose(b, k):
                    pe.wait_ge(p_rdy, BU(layer, b, k // 2))
                    if b > 0 or k >= 2:
                        pe.wait_ge(pt_sb, BK(layer, b, k) - 2)
                    for g in range(4):
                        at = 512 * (k % 2) + 128 * g
                        ins = nc.tensor.transpose(ps[:, 4 + k % 2, 128 * g:128 * g + 128],
                                                  S_sb[:, b % 2, k // 2, at:at + 128], ident[:])
                    ins.then_inc(pt_ps, 1)

                def values(b, k):
                    pe.wait_ge(pt_sb, BK(layer, b, k))
                    if b == 0 and k == 0:
                        pe.wait_ge(v_sb, layer + 1)
                    if b > 0 and k == 0:
                        pe.wait_ge(o_sb, layer * B + b)
                    c, j = k // 2, k % 2
                    for g in range(4):
                        ins = mm(ps[32 * g:32 * g + 32, 6, 128 * c:128 * c + 128], vaug[layer][:, b, 4 * k + g, :],
                                 PT[:, k, 128 * g:128 * g + 128], start=(j == 0), stop=(j == 1),
                                 tile_position=(0, 32 * g))
                    ins.then_inc(o_ps, 1)

                def o_transpose(b):
                    pe.wait_ge(o_sb, BB(layer, b))
                    if layer * B + b > 0:
                        pe.wait_ge(ot_sb, layer * B + b)
                    for c in range(2):
                        ins = nc.tensor.transpose(ps[:, 7, 128 * c:128 * c + 128], osb[:, b % 2, 128 * c:128 * c + 128], ident[:])
                    ins.then_inc(t_ps, 1)

                def a_transpose(b):
                    pe.wait_ge(att_sb, BB(layer, b))
                    nc.tensor.transpose(ps[:, 7, 256:384], att[:, b % 2, :], ident[:]).then_inc(a_ps, 1)

                scores(0, 0)
                scores(0, 1)
                if layer == 1:
                    pe.wait_ge(guard_in, 1)
                    for b in range(B):
                        mm(ps[:, 7, b:b + 1], qT[:, L * b:L * b + L], ksum[:, b:b + 1], start=True, stop=True)
                    mm(ps[:, 7, B:2 * B], wcol(1, "wv")[0:DC, :], ctxsum[:], start=True, stop=True).then_inc(guard_ps, 1)
                    pe.wait_ge(guard_cnt, 1)
                    mm(ps[:, 7, 16:17], ones[:], nan_rows[:], start=True, stop=True).then_inc(guard_tot, 1)
                for b in range(B + 1):
                    if b + 1 < B:
                        scores(b + 1, 0)
                    if b < B:
                        p_transpose(b, 0)
                        p_transpose(b, 1)
                        values(b, 0)
                    if b + 1 < B:
                        scores(b + 1, 1)
                    if b > 0:
                        o_transpose(b - 1)
                    if b < B:
                        p_transpose(b, 2)
                        values(b, 1)
                        p_transpose(b, 3)
                        values(b, 2)
                    if b > 0:
                        a_transpose(b - 1)
                    if b < B:
                        values(b, 3)
                pe.wait_ge(s_wr, 16)
                for half in range(2):
                    pe.wait_ge(ot_sb, BB(layer, 4 * half + 3))
                    for i in range(4):
                        ins = mm(ps[:, 4 + half, 128 * i:128 * i + 128], OT[:, 4 * half + i, :], wcol(layer, "wo"),
                                 start=True, stop=True)
                    ins.then_inc(y_ps, 1)

            pe.wait_ge(s_ctx, 16)
            pe.wait_ge(s_wa, 16)
            k_proj(0, 0)
            v_proj(0, 2)
            pe.wait_ge(pool_const, CONSTS)
            ln_transpose(0)
            q_proj(0)
            pe.wait_ge(v_sb, 1)
            pe.wait_ge(k_sb, 2)
            pe.wait_ge(q_sb, 2)
            attention(0)

            ln_transpose(1)
            for b in range(B):
                if b % 4 == 0:
                    pe.wait_ge(ln_xT, 3 + b // 4)
                ins = mm(ps[:, 6, E * b:E * b + E], xT[:, L * b:L * b + L], wcol(0, "rw"), start=True, stop=True)
            ins.then_inc(lg_ps, 1)
            pe.wait_ge(oh_rdy, 1)
            mm(ps[:, 7, 0:B * E], before[:], oh[:].rearrange("p b e -> p (b e)"), start=True, stop=False)
            for b in range(B - 1):
                mm(ps[:, 7, E * (b + 1):B * E].rearrange("p (b e) -> p b e", e=E), ones_bf[:],
                   oh[:, b:b + 1, :].to_broadcast([P, B - 1 - b, E]), start=False, stop=(b == B - 2))
            for b in range(B):
                ins = mm(ps[:, 7, B * E:B * E + E], ones_bf[:], oh[:, b, :], start=(b == 0), stop=(b == B - 1))
            ins.then_inc(cum_ps, 1)

            pe.wait_ge(slot_rdy, 1)
            k_proj(1, 6)
            pe.wait_ge(k_sb, 4)
            v_proj(1, 6)

            def xs_transpose(t):
                for i, (lo, _) in enumerate(XS_PARTS):
                    if t == lo:
                        pe.wait_ge(xs_in[i], 16)
                if t >= 1:
                    pe.wait_ge(xsT_sb, t)
                nc.tensor.transpose(ps[:, 2, 0:P], xs[:, t, :], ident[:]).then_inc(xsT_ps, 1)

            def up(t):
                pe.wait_ge(xsT_sb, t + 1)
                pe.wait_ge(fc_rdy, t + 1)
                if t >= 2:
                    pe.wait_ge(h_relu, t - 1)
                for c in range(C0):
                    ins = mm(ps[:, t % 2, P * c:P * c + P], fcb[:, t % 2, P * c:P * c + P], xsT[:, t % 2, :],
                             start=True, stop=True)
                ins.then_inc(h_ps, 1)

            def down(t):
                expert = pe.value_load(eid[0:1, t:t + 1], min_val=0, max_val=E - 1)
                pe.wait_ge(h_sq, t + 1)
                if t >= 1:
                    pe.wait_ge(yt_sb, t)
                for c in range(C0):
                    ins = mm(ps[:, 3, 0:D], h2[:, t % 2, P * c:P * c + P],
                             proj[:, bass.ds(expert, 1), c, :].rearrange("p a d -> p (a d)"),
                             start=(c == 0), stop=(c == C0 - 1))
                ins.then_inc(yt_ps, 1)

            xs_transpose(0)
            pe.wait_ge(eid_rdy, 1)
            for t in range(TILES):
                if t + 1 < TILES:
                    xs_transpose(t + 1)
                up(t)
                if t >= 1:
                    down(t - 1)
            down(TILES - 1)

            pe.wait_ge(v_sb, 2)
            ln_transpose(2)
            q_proj(1)
            pe.wait_ge(kmask_dma, 16 * H)
            pe.wait_ge(q_sb, 4)
            attention(1)
            ln_transpose(3)
            for b in range(B):
                if b % 4 == 0:
                    pe.wait_ge(ln_xT, 7 + b // 4)
                ins = mm(ps[:, 6, E * b:E * b + E], xT[:, L * b:L * b + L], wcol(1, "wg"), start=True, stop=True)
            ins.then_inc(lg1_ps, 1)

            def expert_up(e, half):
                if half == 0:
                    pe.wait_ge(s_w12[e % 2], 32 * (e // 2 + 1))
                if e > 0:
                    pe.wait_ge(hT_rdy, (2 * (e - 1) + half + 1) * C1)
                for c in range(C1):
                    mm(ps[:, 2 * half + c, :], w1[:, e % 2, P * c:P * c + P], xT[:, 512 * half:512 * half + 512],
                       start=True, stop=True).then_inc(up_ps, 1)

            def expert_down(e, half):
                pe.wait_ge(hT_rdy, (2 * e + half + 1) * C1)
                if e > 0:
                    pe.wait_ge(x_exp, 2 * (e - 1) + half + 1)
                for i in range(4):
                    for c in range(C1):
                        ins = mm(ps[:, 4 + half, P * i:P * i + P], hT[:, half, c, P * i:P * i + P], w2[:, e % 2, c, :],
                                 start=(c == 0), stop=(c == C1 - 1))
                ins.then_inc(dn_ps, 1)

            expert_up(0, 0)
            expert_up(0, 1)
            pe.wait_ge(gates_rdy, 1)
            for b in range(B):
                ins = nc.tensor.transpose(ps[0:E, 6 + b // 4, L * (b % 4):L * (b % 4) + L], gates[:, b, :], ident[:])
            ins.then_inc(gT_ps, 1)
            pe.wait_ge(gT_sb, 1)
            pe.wait_ge(s_b2, 16)
            for b in range(B):
                ins = mm(ps[:, 6 + b // 4, D * (b % 4):D * (b % 4) + D], gT[:, b, :], b2[:], start=True, stop=True)
            ins.then_inc(b2_ps, 1)
            for e in range(E):
                for half in range(2):
                    expert_down(e, half)
                    if e + 1 < E:
                        expert_up(e + 1, half)


_OUT = (8, 128, 128)


def kernel(**inputs):
    import numpy as np
    import concourse.bacc as bacc
    from concourse.bass_utils import run_bass_kernel_spmd

    def get(name):
        return np.asarray(inputs[name])

    def rows(a):
        out = np.zeros((P, a.shape[1]), a.dtype)
        out[:a.shape[0]] = a
        return out

    def spread(a):
        return np.broadcast_to(a[None, :], (P, a.shape[0]))

    vperm = np.array([DH * (8 * c + 4 * j + g) + d for c in range(2) for g in range(4) for j in range(2) for d in range(DH)])
    kv = get("L0_xattn_Wkv").reshape(H, 2, DH, DC)
    bkv = get("L0_xattn_bkv").reshape(H, 2, DH)
    layer0 = dict(
        wk=rows(kv[:, 0].reshape(D, DC).T), wv=rows(kv[:, 1].reshape(D, DC)[vperm].T), wq=get("L0_xattn_Wq").T,
        bq=get("L0_xattn_bq")[:, None], bk=bkv[:, 0].reshape(D, 1), bv=bkv[:, 1].reshape(D)[vperm][:, None])
    rest = dict(
        wo0=get("L0_xattn_Wo").T[vperm], bo0=spread(get("L0_xattn_bo")), rw=get("L0_ffn_router_w").T,
        wk=rows(get("L1_xattn_Wk")), wv=rows(get("L1_xattn_Wv")[:, vperm]), wq=get("L1_xattn_Wq"),
        bq=get("L1_xattn_bq")[:, None], bk=get("L1_xattn_bk")[:, None], bv=get("L1_xattn_bv")[vperm][:, None],
        wo1=get("L1_xattn_Wo")[vperm], bo1=spread(get("L1_xattn_bo")), wg=get("L1_ffn_Wg"), bg=spread(get("L1_ffn_bg")))
    arrays = dict(
        x=get("x").reshape(N, D),
        ctxT=get("ctx_768").reshape(B * M, DC).T,
        wa=np.concatenate([layer0[n] for n in A_COLS], axis=1),
        wr=np.concatenate([rest[n] for n in R_COLS], axis=1),
        fc=get("L0_ffn_expert_fc").transpose(1, 0, 2),
        proj=get("L0_ffn_expert_proj").reshape(E, D, C0, P).transpose(3, 0, 2, 1),
        w1=np.concatenate([get("L1_ffn_W1"), get("L1_ffn_b1").reshape(E, C1, P).transpose(0, 2, 1)], axis=2),
        w2=get("L1_ffn_W2").reshape(E, C1, P, D).transpose(0, 2, 1, 3),
        b2=get("L1_ffn_b2"))
    nc = bacc.Bacc("TRN2", target_bir_lowering=False, num_devices=1)
    in_map, args = {}, []
    for name, a in arrays.items():
        in_map["in_" + name] = np.ascontiguousarray(a)
        args.append(nc.dram_tensor("in_" + name, in_map["in_" + name].shape, mybir.dt.from_np(in_map["in_" + name].dtype), kind="ExternalInput").ap())
    out = nc.dram_tensor("out", (N, D), mybir.dt.float32, kind="ExternalOutput").ap()
    build(nc, *args, out)
    result = run_bass_kernel_spmd(nc, [in_map], core_ids=[0])
    return result.results[0]["out"].reshape(_OUT)
```

```python
import concourse.bass as bass
from concourse import mybir
from contextlib import ExitStack

B, L, D = 8, 128, 128
M, DC = 128, 96
H, DH = 16, 8
E = 8
F0, F1 = 4 * D, 2 * D
N = B * L
P = 128
C0, C1 = F0 // P, F1 // P
TILES = (N + E * (P - 1)) // P
XS_PARTS = [(0, 2), (2, 8), (8, TILES)]
SCALE = float(DH) ** -0.5
CLAMP = 10000.0 / SCALE
TEMP = 5.0
GATE_EPS = 1e-9
LN_EPS = 1e-5

A_COLS = dict(wk=512, wv=128, bk=4, bkl=4, bv=1, bq=4, bql=4, wq=512)
R_COLS = dict(wo0=128, bo0=128, rw=8, wk=512, wv=128, wq=512, bq=4, bql=4, bk=4, bkl=4, bv=1, wo1=128, bo1=128,
              wg=8, bg=8)
A_FIRST = 512 + 128 + 4 + 4 + 1


def columns(sizes):
    at, out = 0, {}
    for name, n in sizes.items():
        out[name] = (at, at + n)
        at += n
    return out, at


A_AT, A_N = columns(A_COLS)
R_AT, R_N = columns(R_COLS)


def build(nc, x_in, ctx_in, wa_in, wr_in, fc_in, proj_in, w1_in, w2_in, b2_in, out):
    fp32, bf16, i32 = mybir.dt.float32, mybir.dt.bfloat16, mybir.dt.int32
    ALU, ACT, AX = mybir.AluOpType, mybir.ActivationFunctionType, mybir.AxisListType.X
    AXY = mybir.AxisListType.XY

    slots_x = nc.dram_tensor("slots_x", (TILES * P, D), fp32, kind="Internal").ap()
    slots_y = nc.dram_tensor("slots_y", (TILES * P, D), fp32, kind="Internal").ap()

    ctx = ExitStack()
    with ctx:
        def sb(name, shape, dt=fp32):
            return ctx.enter_context(nc.sbuf_tensor(name, shape, dt))

        def sem(name):
            return ctx.enter_context(nc.semaphore(name))

        ident = sb("ident", [P, P])
        ones_bf = sb("ones_bf", [P, P], bf16)
        ones = sb("ones", [P, P])
        before = sb("before", [P, P], bf16)
        head_rows = sb("head_rows", [P, 4])
        lo_q = sb("lo_q", [P, 1])
        lo_k = sb("lo_k", [P, 1])
        zeros = sb("zeros", [P, D])
        minus_half = sb("minus_half", [P, B])
        rank_down = sb("rank_down", [P, E])
        upto = sb("upto", [P, E, E])
        tile_no = sb("tile_no", [P, TILES])

        wa = sb("wa", [P, A_N])
        wr = sb("wr", [P, R_N])
        ctxT = sb("ctxT", [DC, B * M])
        fc = sb("fc", [P, E, F0])
        proj = sb("proj", [P, E, C0, D])
        w1 = sb("w1", [P, 2, F1 + C1])
        w2 = sb("w2", [P, 2, C1, D])
        b2 = sb("b2", [E, D])

        def wcol(layer, name):
            if layer == 0 and name in A_AT:
                lo, hi = A_AT[name]
                return wa[:, lo:hi]
            lo, hi = R_AT[name + str(layer) if name in ("wo", "bo") else name]
            return wr[:, lo:hi]

        xr = sb("xr", [P, B, D])
        xn = sb("xn", [P, B, D])
        xT = sb("xT", [P, N])
        f32r = mybir.dt.float32r
        qk4 = sb("qk4", [P, 4, N], f32r)
        k4 = [fc[:].rearrange("p e f -> p (e f)").rearrange("p (k n) -> p k n", k=4).bitcast(f32r), qk4]
        split = sb("split", [P, 2, 512], f32r)
        kmask = sb("kmask", [P, 4, B, 4, M], f32r)
        vaug = sb("vaug", [P, B, H, 32])
        work = sb("work", [P, 4096])
        work2 = sb("work2", [P, 2048])
        S_sb = work[:].rearrange("p (b u n) -> p b u n", b=2, u=2)
        mx = sb("mx", [P, B, H])
        PT = work2[:].rearrange("p (k n) -> p k n", k=4)
        osb = sb("osb", [P, 2, 256])
        rc = sb("rc", [P, 2, H])
        att = sb("att", [P, 2, D])
        OT = sb("OT", [P, B, L])
        stats = sb("stats", [P, B, 6])
        mv = sb("mv", [P, B, 2])
        ve = sb("ve", [P, B])
        rstd = sb("rstd", [P, B])
        qk_sums = sb("qk_sums", [P, 16])
        ctxsum = sb("ctxsum", [DC, B])
        vmean = sb("vmean", [P, B])
        tn2 = sb("tn2", [P, 16])
        nan_rows = sb("nan_rows", [P, 1])
        nan_any = sb("nan_any", [P, 1], i32)
        lg = sb("lg", [P, B, E])
        lgm = sb("lgm", [P, B])
        eq = sb("eq", [P, B, E])
        oh = sb("oh", [P, B, E], bf16)
        oh2 = sb("oh2", [P, B, E])
        tiles_i = sb("tiles_i", [P, E], i32)
        tiles_f = sb("tiles_f", [P, E])
        upsel = sb("upsel", [P, E, E])
        ends = sb("ends", [P, E])
        base = sb("base", [P, E])
        slot_f = sb("slot_f", [P, B])
        slot_i = sb("slot_i", [P, B], i32)
        cmp = sb("cmp", [P, TILES, E])
        eid_f = sb("eid_f", [P, TILES])
        eid = sb("eid", [P, TILES], i32)
        xs = work[:, 0:TILES * D].rearrange("p (t d) -> p t d", d=D)
        xsT = sb("xsT", [P, 2, P])
        fcb = work[:, 2048:3072].rearrange("p (t f) -> p t f", t=2)
        hr = work[:, 3072:4096].rearrange("p (t f) -> p t f", t=2)
        h2 = work2[:, 0:1024].rearrange("p (t f) -> p t f", t=2)
        ys = sb("ys", [P, 2, D])
        yg = work2[:, 1024:2048].rearrange("p (b d) -> p b d", d=D)
        pr = sb("pr", [P, B, E])
        p2 = sb("p2", [P, B, E])
        m1 = sb("m1", [P, B])
        m2 = sb("m2", [P, B])
        gsum = sb("gsum", [P, B])
        gates = sb("gates", [P, B, E])
        gT = sb("gT", [E, B, L])
        hT = work2[:].rearrange("p (h c n) -> p h c n", h=2, c=C1)

        ps = ctx.enter_context(nc.psum_tensor("ps", [P, 8, 512], fp32))

        s_x, s_ctx, s_wa, s_wq, s_wr = sem("s_x"), sem("s_ctx"), sem("s_wa"), sem("s_wq"), sem("s_wr")
        qk_hi = sem("qk_hi")
        s_fc, s_b2, s_zero = sem("s_fc"), sem("s_b2"), sem("s_zero")
        s_w12 = [sem("s_w12_0"), sem("s_w12_1")]
        pool_const = sem("pool_const")
        dve_const = sem("dve_const")
        dve_chain, act_chain, pool_chain = sem("dve_chain"), sem("act_chain"), sem("pool_chain")
        ln_var, ln_rstd, ln_norm, ln_tr, ln_xT = (sem(n) for n in ("ln_var", "ln_rstd", "ln_norm", "ln_tr", "ln_xT"))
        bo_added = sem("bo_added")
        k_ps, k_sb, v_ps, v_sb, q_ps, q_sb = (sem(n) for n in ("k_ps", "k_sb", "v_ps", "v_sb", "q_ps", "q_sb"))
        kmask_dve, kmask_act, kmask_dma = sem("kmask_dve"), sem("kmask_act"), sem("kmask_dma")
        guard_in, guard_cnt, guard_tot = (
            sem(n) for n in ("guard_in", "guard_cnt", "guard_tot"))
        s_ps, s_sub, p_rdy, pt_ps, pt_sb, o_ps, o_sb, t_ps, att_sb, a_ps, ot_sb, y_ps, x_attn = (
            sem(n) for n in ("s_ps", "s_sub", "p_rdy", "pt_ps", "pt_sb", "o_ps", "o_sb", "t_ps", "att_sb",
                             "a_ps", "ot_sb", "y_ps", "x_attn"))
        lg_ps, oh_rdy, cum_ps, slot_rdy, eid_rdy = (
            sem(n) for n in ("lg_ps", "oh_rdy", "cum_ps", "slot_rdy", "eid_rdy"))
        scattered, xsT_ps, xsT_sb, fc_rdy, h_ps, h_relu, h_sq, yt_ps, yt_sb = (
            sem(n) for n in ("scattered", "xsT_ps", "xsT_sb", "fc_rdy", "h_ps", "h_relu", "h_sq", "yt_ps", "yt_sb"))
        lg1_ps, lg1_sub, lg1_exp, gates_rdy, gT_ps, gT_sb, b2_ps, b2_added = (
            sem(n) for n in ("lg1_ps", "lg1_sub", "lg1_exp", "gates_rdy", "gT_ps", "gT_sb", "b2_ps", "b2_added"))
        up_ps, hT_rdy, dn_ps, x_exp = (sem(n) for n in ("up_ps", "hT_rdy", "dn_ps", "x_exp"))
        s_out = sem("s_out")

        xs_in = [sem(f"xs_in{i}") for i in range(len(XS_PARTS))]
        y_out = [sem(f"y_out{i}") for i in range(2)]
        gathered = [sem(f"gathered{b}") for b in range(B)]

        CONSTS = 6
        BU = lambda l, b, u: (l * B + b) * 2 + u + 1
        BK = lambda l, b, k: (l * B + b) * 4 + k + 1
        BB = lambda l, b: l * B + b + 1

        block = ctx.enter_context(nc.Block())

        @block.sync
        def _(sp):
            sp.dma_start(ctxT[:], ctx_in).then_inc(s_ctx, 16)
            sp.dma_start(wa[:, 0:A_FIRST], wa_in[:, 0:A_FIRST]).then_inc(s_wa, 16)
            sp.dma_start(wa[:, A_FIRST:A_N], wa_in[:, A_FIRST:A_N]).then_inc(s_wq, 16)
            sp.dma_start(wr[:], wr_in).then_inc(s_wr, 16)
            sp.dma_start(proj[:], proj_in).then_inc(s_fc, 16)
            sp.dma_start(b2[:], b2_in).then_inc(s_b2, 16)
            sp.dma_start(w1[:, 0, :], w1_in[0]).then_inc(s_w12[0], 16)
            sp.dma_start(w2[:, 0], w2_in[0]).then_inc(s_w12[0], 16)
            sp.dma_start(w1[:, 1, :], w1_in[1]).then_inc(s_w12[1], 16)
            sp.dma_start(w2[:, 1], w2_in[1]).then_inc(s_w12[1], 16)
            sp.wait_ge(pool_const, CONSTS)
            sp.dma_start(slots_x.rearrange("(t p) d -> p t d", p=P),
                         zeros[:].unsqueeze(1).to_broadcast([P, TILES, D])).then_inc(s_zero, 16)

            sp.wait_ge(kmask_dve, 2)
            sp.wait_ge(kmask_act, 2)
            sp.dma_start(fc[:], fc_in).then_inc(s_fc, 16)

            sp.wait_ge(scattered, 16 * B)
            for i, (lo, hi) in enumerate(XS_PARTS):
                sp.dma_start(xs[:, lo:hi, :], slots_x.rearrange("(t p) d -> p t d", p=P)[:, lo:hi, :]).then_inc(xs_in[i], 16)
            sp.wait_ge(k_sb, 16)
            sp.wait_ge(s_ps, BU(0, B - 1, 1))

            def keys_in(i):
                sp.dma_start(kmask[DH * i:DH * (i + 1), :, :, i % 4, :].rearrange("p k b m -> p (k b) m").bitcast(fp32),
                             k4[1][DH * i:DH * (i + 1), :, :].rearrange("p k (b m) -> p (k b) m", m=M).bitcast(fp32))\
                    .then_inc(kmask_dma, 16)

            keys_in(H - 1)
            for t in range(TILES):
                keys_in(t)
                sp.wait_ge(yt_sb, t + 1)
                sp.dma_start(slots_y[t * P:(t + 1) * P, :], ys[:, t % 2, :]).then_inc(y_out[t % 2], 16)

            for e in range(2, E):
                sp.wait_ge(dn_ps, 2 * (e - 1))
                sp.dma_start(w1[:, e % 2, :], w1_in[e]).then_inc(s_w12[e % 2], 16)
                sp.dma_start(w2[:, e % 2], w2_in[e]).then_inc(s_w12[e % 2], 16)
            for half in range(2):
                sp.wait_ge(x_exp, 2 * (E - 1) + half + 1)
                sp.dma_start(out.rearrange("(b t) d -> t b d", t=L)[:, 4 * half:4 * half + 4, :],
                             xr[:, 4 * half:4 * half + 4, :]).then_inc(s_out, 16)
            sp.wait_ge(s_out, 32)

        @block.gpsimd
        def _(pool):
            count = [0]

            def link(ins):
                count[0] += 1
                ins.then_inc(pool_chain, 1)
                pool.wait_ge(pool_chain, count[0])

            link(nc.gpsimd.memset(ones[:], 1.0))
            nc.gpsimd.affine_select(out=ident[:], in_=ones[:], pattern=[[-1, P]], compare_op=ALU.is_equal,
                                    fill=0.0, base=0, channel_multiplier=1).then_inc(pool_const, 1)
            nc.gpsimd.memset(minus_half[:], -0.5).then_inc(pool_const, 1)
            nc.gpsimd.memset(zeros[:], 0.0).then_inc(pool_const, 1)
            nc.gpsimd.iota(rank_down[:], pattern=[[-1, E]], base=E, channel_multiplier=0,
                           allow_small_or_imprecise_dtypes=True).then_inc(pool_const, 1)
            nc.gpsimd.iota(tile_no[:], pattern=[[1, TILES]], base=0, channel_multiplier=0,
                           allow_small_or_imprecise_dtypes=True).then_inc(pool_const, 1)
            link(nc.gpsimd.memset(upto[:], 1.0))
            nc.gpsimd.affine_select(out=upto[:], in_=upto[:], pattern=[[1, E], [-1, E]], compare_op=ALU.is_ge,
                                    fill=0.0, base=0, channel_multiplier=0).then_inc(pool_const, 1)
            link(nc.gpsimd.memset(ones_bf[:], 1.0))
            link(nc.gpsimd.affine_select(out=before[:], in_=ones_bf[:], pattern=[[1, P]], compare_op=ALU.is_gt,
                                         fill=0.0, base=0, channel_multiplier=-1))

            def rsqrt(k, half):
                pool.wait_ge(ln_var, 2 * k + half + 1)
                sl = slice(4 * half, 4 * half + 4)
                nc.gpsimd.tensor_tensor(rstd[:, sl], ve[:, sl], minus_half[:, sl], ALU.pow).then_inc(ln_rstd, 1)

            def add_bo(layer, k):
                pool.wait_ge(s_wr, 16)
                for half in range(2):
                    pool.wait_ge(ln_norm, 2 * k + half + 1)
                    sl = slice(4 * half, 4 * half + 4)
                    nc.gpsimd.tensor_tensor(xr[:, sl, :], xr[:, sl, :],
                                            wcol(layer, "bo").unsqueeze(1).to_broadcast([P, 4, D]),
                                            ALU.add).then_inc(bo_added, 1)

            rsqrt(0, 0)
            rsqrt(0, 1)
            add_bo(0, 0)
            rsqrt(1, 0)
            rsqrt(1, 1)
            pool.wait_ge(slot_rdy, 1)
            pool.wait_ge(s_zero, 16)
            pool.wait_ge(ln_norm, 4)
            for b in range(B):
                pool.indirect_dma_start(slots_x, bass.IndirectOffsetOnAxis(slot_i[:, b:b + 1], 0),
                                        xn[:, b, :], None).then_inc(scattered, 16)
            pool.wait_ge(y_out[0], 16 * ((TILES + 1) // 2))
            pool.wait_ge(y_out[1], 16 * (TILES // 2))
            for b in range(B):
                pool.indirect_dma_start(yg[:, b, :], None, slots_y,
                                        bass.IndirectOffsetOnAxis(slot_i[:, b:b + 1], 0)).then_inc(gathered[b], 16)
                if b == 5:
                    rsqrt(2, 0)
            rsqrt(2, 1)
            add_bo(1, 2)
            rsqrt(3, 0)
            rsqrt(3, 1)

        @block.scalar
        def _(act):
            act.dma_start(xr[:], x_in.rearrange("(b t) d -> t b d", t=L)).then_inc(s_x, 16)
            count = [0]

            def link(ins):
                count[0] += 1
                ins.then_inc(act_chain, 1)
                act.wait_ge(act_chain, count[0])

            def ln_evac(k):
                for half in range(2):
                    act.wait_ge(ln_tr, 2 * k + half + 1)
                    if k == 1 and half == 0:
                        act.wait_ge(q_ps, 8)
                    if k == 2 and half == 0:
                        act.wait_ge(lg_ps, 1)
                    if k == 3 and half == 0:
                        act.wait_ge(q_ps, 16)
                    nc.scalar.activation(xT[:, 512 * half:512 * half + 512], ps[:, 4 + half, :], ACT.Copy).then_inc(ln_xT, 1)

            def hi_parts(layer, is_k, bank):
                produced = k_ps if is_k else q_ps
                mask, bias = (lo_k, wcol(layer, "bkl")) if is_k else (lo_q, wcol(layer, "bql"))
                for i in range(8):
                    act.wait_ge(produced, 8 * layer + i + 1)
                    n = 16 * layer + (0 if is_k else 8) + i
                    if n >= 2:
                        of_q, before_layer, at = (n - 2) // 8 % 2, (n - 2) // 16, (n - 2) % 8
                        act.wait_ge(q_sb if of_q else k_sb, 8 * before_layer + at + 1)
                    nc.scalar.activation(split[:, n % 2, :], ps[:, bank + i % 4, :], ACT.Identity,
                                         scale=mask[:, 0:1], bias=bias[:, i % 4:i % 4 + 1],
                                         accum_out=qk_sums[:, n % 16:n % 16 + 1]).then_inc(qk_hi, 1)

            def attention(layer):
                def exp(b, u):
                    act.wait_ge(s_sub, BU(layer, b, u))
                    z = S_sb[:, b % 2, u, :]
                    if layer == 0:
                        nc.scalar.activation(z, z, ACT.Exp, scale=SCALE).then_inc(p_rdy, 1)
                    else:
                        link(nc.scalar.activation(z, z, ACT.Relu, scale=-1.0))
                        nc.scalar.activation(z, z, ACT.Exp, scale=-SCALE).then_inc(p_rdy, 1)

                def pt_evac(b, k):
                    act.wait_ge(pt_ps, BK(layer, b, k))
                    if layer + b > 0:
                        act.wait_ge(o_ps, 4 * (layer * B + b - 1) + k + 1)
                    nc.scalar.activation(PT[:, k, :], ps[:, 4 + k % 2, :], ACT.Copy).then_inc(pt_sb, 1)

                def o_evac(b):
                    act.wait_ge(o_ps, 4 * (layer * B + b) + 4)
                    if layer * B + b >= 2:
                        act.wait_ge(t_ps, layer * B + b - 1)
                    nc.scalar.activation(osb[:, b % 2, :], ps[:, 6, 0:256], ACT.Copy).then_inc(o_sb, 1)

                exp(0, 0)
                exp(0, 1)
                for b in range(B):
                    for u in range(2):
                        pt_evac(b, 2 * u)
                        pt_evac(b, 2 * u + 1)
                        if b + 1 < B:
                            exp(b + 1, u)
                    o_evac(b)

            act.wait_ge(s_wa, 16)
            act.wait_ge(dve_const, 1)
            hi_parts(0, True, 0)
            ln_evac(0)
            for half in range(2):
                act.wait_ge(k_sb, 4 * half + 4)
                for k in range(4):
                    for g in range(2, 4):
                        ins = nc.scalar.activation(kmask[:, k, 4 * half:4 * half + 4, g, :],
                                                   k4[0][:, k, 512 * half:512 * half + 512].bitcast(fp32)
                                                   .rearrange("p (b m) -> p b m", m=M),
                                                   ACT.Copy, scale=head_rows[:, g:g + 1])
                ins.then_inc(kmask_act, 1)
                if half == 0:
                    act.wait_ge(s_wq, 16)
                    hi_parts(0, False, 0)
            attention(0)

            ln_evac(1)
            def fc_copy(t):
                expert = act.value_load(eid[0:1, t:t + 1], min_val=0, max_val=E - 1)
                if t >= 2:
                    act.wait_ge(h_ps, t - 1)
                nc.scalar.activation(fcb[:, t % 2, :], fc[:, bass.ds(expert, 1), :].rearrange("p a f -> p (a f)"),
                                     ACT.Copy).then_inc(fc_rdy, 1)

            hi_parts(1, True, 4)
            act.wait_ge(eid_rdy, 1)
            act.wait_ge(s_fc, 32)
            fc_copy(0)
            fc_copy(1)
            for t in range(TILES):
                act.wait_ge(h_ps, t + 1)
                if t >= 2:
                    act.wait_ge(h_sq, t - 1)
                nc.scalar.activation(hr[:, t % 2, :], ps[:, t % 2, :], ACT.Relu).then_inc(h_relu, 1)
                if t + 2 < TILES:
                    fc_copy(t + 2)

            ln_evac(2)
            hi_parts(1, False, 0)
            attention(1)
            ln_evac(3)
            act.wait_ge(lg1_sub, 1)
            nc.scalar.activation(pr[:], lg[:], ACT.Exp, scale=1.0 / TEMP).then_inc(lg1_exp, 1)

            def gates_evac():
                act.wait_ge(gT_ps, 1)
                nc.scalar.activation(gT[:].rearrange("p b l -> p (b l)"), ps[0:E, 6:8, :].rearrange("p a n -> p (a n)"),
                                     ACT.Copy).then_inc(gT_sb, 1)

            for e in range(E):
                act.wait_ge(s_w12[e % 2], 32 * (e // 2 + 1))
                for half in range(2):
                    for c in range(C1):
                        act.wait_ge(up_ps, (2 * e + half) * C1 + c + 1)
                        if e > 0:
                            act.wait_ge(dn_ps, 2 * (e - 1) + half + 1)
                        nc.scalar.activation(hT[:, half, c, :], ps[:, 2 * half + c, :], ACT.Gelu,
                                             bias=w1[:, e % 2, F1 + c:F1 + c + 1]).then_inc(hT_rdy, 1)
                if e == 2:
                    gates_evac()

        @block.vector
        def _(dve):
            count = [0]

            def link(ins):
                count[0] += 1
                ins.then_inc(dve_chain, 1)
                dve.wait_ge(dve_chain, count[0])

            def ln_stats(k, half):
                bs = range(4 * half, 4 * half + 4)
                sl = slice(4 * half, 4 * half + 4)
                for b in bs:
                    ins = nc.vector.bn_stats(stats[:, b, :], xr[:, b, :])
                link(ins)
                for b in bs:
                    ins = nc.vector.bn_aggr(mv[:, b, :], stats[:, b, :])
                link(ins)
                nc.vector.tensor_scalar(ve[:, sl], mv[:, sl, 1], LN_EPS, None, ALU.add).then_inc(ln_var, 1)

            def ln_normalise(k, half):
                dve.wait_ge(ln_rstd, 2 * k + half + 1)
                if k == 2 and half == 0:
                    dve.wait_ge(scattered, 16 * B)
                if k in (1, 3) and half == 0:
                    dve.wait_ge(ln_tr, 2 * k)
                for b in range(4 * half, 4 * half + 4):
                    ins = nc.vector.tensor_scalar(xn[:, b, :], xr[:, b, :], mv[:, b, 0:1], rstd[:, b:b + 1],
                                                  ALU.subtract, ALU.mult)
                ins.then_inc(ln_norm, 1)

            def v_evac(layer, bank):
                dve.wait_ge(v_ps, layer + 1)
                src = ps[:, bank:bank + 2, :].rearrange("p k (q g x) -> p (k q) g x", g=4, x=16)
                dst = vaug[:].rearrange("p b (c j g) x -> p (b c) j g x", c=2, j=2)
                for j in range(2):
                    ins = nc.vector.tensor_copy(dst[:, :, j, :, 8 * j:8 * j + 8], src[:, :, :, 8 * j:8 * j + 8])
                ins.then_inc(v_sb, 1)

            def attention(layer):
                def scores(b, u):
                    dve.wait_ge(s_ps, BU(layer, b, u))
                    s = ps[:, 2 * u:2 * u + 2, :].rearrange("p k (h m) -> p (k h) m", m=M)
                    top = mx[:, b, 8 * u:8 * u + 8]
                    link(nc.vector.tensor_reduce(top, s, axis=AX, op=ALU.max))
                    if layer == 1:
                        link(nc.vector.tensor_scalar(top, top, -CLAMP, CLAMP, ALU.max, ALU.min))
                    if b >= 2:
                        dve.wait_ge(pt_ps, BK(layer, b - 2, 2 * u + 1))
                    z = S_sb[:, b % 2, u, :].rearrange("p (h m) -> p h m", m=M)
                    topb = top.unsqueeze(2).to_broadcast([P, 8, M])
                    if layer == 0:
                        ins = nc.vector.tensor_tensor(z, s, topb, ALU.subtract)
                    else:
                        ins = nc.vector.scalar_tensor_tensor(z, s, -CLAMP, topb, ALU.max, ALU.subtract)
                    ins.then_inc(s_sub, 1)

                def norm(b):
                    dve.wait_ge(t_ps, BB(layer, b))
                    t = ps[:, 7, 0:256].rearrange("p (q x) -> p q x", x=32)
                    link(nc.vector.reciprocal(rc[:, b % 2, :].rearrange("p (q j) -> p q j", j=2), t[:, :, 16:18]))
                    if layer * B + b >= 2:
                        dve.wait_ge(a_ps, layer * B + b - 1)
                    nc.vector.tensor_tensor(
                        att[:, b % 2, :].rearrange("p (q j d) -> p q j d", j=2, d=DH),
                        t[:, :, 0:16].rearrange("p q (j d) -> p q j d", d=DH),
                        rc[:, b % 2, :].rearrange("p (q j) -> p q j", j=2).unsqueeze(3).to_broadcast([P, 8, 2, DH]),
                        ALU.mult).then_inc(att_sb, 1)

                def ot(b):
                    dve.wait_ge(a_ps, BB(layer, b))
                    ins = nc.vector.tensor_scalar(OT[:, b, :], ps[:, 7, 256:384], wcol(layer, "bv"), None, ALU.add)
                    if layer == 1:
                        link(ins)
                        ins = nc.vector.copy_predicated(OT[:, b, :], nan_any[:, 0:1].to_broadcast([P, L]),
                                                        vmean[:, b:b + 1].to_broadcast([P, L]))
                    ins.then_inc(ot_sb, 1)

                def add_and_stats(half):
                    dve.wait_ge(y_ps, 2 * layer + half + 1)
                    dve.wait_ge(bo_added, 2 * layer + half + 1)
                    sl = slice(4 * half, 4 * half + 4)
                    link(nc.vector.tensor_tensor(xr[:, sl, :], ps[:, half, :].rearrange("p (b d) -> p b d", b=4),
                                                 xr[:, sl, :], ALU.add))
                    ln_stats(2 * layer + 1, half)

                scores(0, 0)
                scores(0, 1)
                if layer == 1:
                    guard()
                for b in range(B + 1):
                    if b + 1 < B:
                        scores(b + 1, 0)
                    if b > 0:
                        norm(b - 1)
                    if b + 1 < B:
                        scores(b + 1, 1)
                    if b > 0:
                        ot(b - 1)
                    if b == B - 1:
                        add_and_stats(0)
                ln_normalise(2 * layer + 1, 0)
                add_and_stats(1)
                ln_normalise(2 * layer + 1, 1)

            def guard():
                link(nc.vector.tensor_tensor(tn2[:], qk_sums[:], qk_sums[:], ALU.not_equal))
                nc.vector.tensor_reduce(nan_rows[:], tn2[:], axis=AX, op=ALU.add).then_inc(guard_cnt, 1)
                dve.wait_ge(guard_tot, 1)
                nc.vector.tensor_scalar(vmean[:], ps[:, 7, B:2 * B], 1.0 / M, wcol(1, "bv"), ALU.mult, ALU.add)
                link(nc.vector.tensor_scalar(nan_any[:], ps[:, 7, 16:17], 0.5, None, ALU.is_gt))

            def parts(layer, is_k, bank):
                bias = wcol(layer, "bk" if is_k else "bq")
                dst = k4[layer] if is_k else qk4
                for i in range(8):
                    n = 16 * layer + (0 if is_k else 8) + i
                    dve.wait_ge(qk_hi, n + 1)
                    if n == 24:
                        dve.wait_ge(kmask_dma, 16 * H)
                    if n == 16:
                        dve.wait_ge(s_ps, BU(0, B - 1, 1))
                    half, k = i // 4, i % 4
                    nc.vector.scalar_tensor_tensor(dst[:, k, 512 * half:512 * half + 512], ps[:, bank + k, :],
                                                   bias[:, k:k + 1], split[:, n % 2, :].bitcast(fp32),
                                                   ALU.add, ALU.subtract).then_inc(k_sb if is_k else q_sb, 1)

            def first_max(src, top, onehot):
                link(nc.vector.tensor_reduce(top[:], src[:], axis=AX, op=ALU.max))
                link(nc.vector.tensor_tensor(eq[:], src[:], top[:].unsqueeze(2).to_broadcast([P, B, E]), ALU.is_equal))
                link(nc.vector.tensor_tensor(eq[:], eq[:], rank_down[:].unsqueeze(1).to_broadcast([P, B, E]), ALU.mult))
                link(nc.vector.tensor_reduce(lgm[:], eq[:], axis=AX, op=ALU.max))
                return nc.vector.tensor_tensor(onehot[:], eq[:], lgm[:].unsqueeze(2).to_broadcast([P, B, E]), ALU.is_equal)

            link(nc.vector.memset(vaug[:], 0.0))
            va = vaug[:].rearrange("p b (c j g) x -> p (b c) j g x", c=2, j=2)
            for j in range(2):
                nc.vector.memset(va[:, :, j, :, 16 + j:17 + j], 1.0)
            dve.wait_ge(pool_const, 1)
            nc.vector.tensor_reduce(head_rows[:], ident[:].rearrange("p (t g d) -> p g t d", t=4, g=4), axis=AXY,
                                    op=ALU.add)
            nc.vector.tensor_reduce(lo_q[:], ident[:, 64:128], axis=AX, op=ALU.add)
            nc.vector.tensor_reduce(lo_k[:], ident[:].rearrange("p (a t r) -> p t a r", a=2, t=2)[:, 1], axis=AXY,
                                    op=ALU.add).then_inc(dve_const, 1)
            dve.wait_ge(dve_const, 1)
            dve.wait_ge(s_x, 16)
            ln_stats(0, 0)
            ln_stats(0, 1)
            dve.wait_ge(s_wa, 16)
            parts(0, True, 0)
            ln_normalise(0, 0)
            ln_normalise(0, 1)
            for half in range(2):
                for k in range(4):
                    for g in range(2):
                        ins = nc.vector.tensor_scalar(kmask[:, k, 4 * half:4 * half + 4, g, :],
                                                      k4[0][:, k, 512 * half:512 * half + 512].bitcast(fp32)
                                                      .rearrange("p (b m) -> p b m", m=M),
                                                      head_rows[:, g:g + 1], None, ALU.mult)
                ins.then_inc(kmask_dve, 1)
                if half == 0:
                    v_evac(0, 6)
                    dve.wait_ge(s_wq, 16)
                    parts(0, False, 0)
            dve.wait_ge(s_wa, 16)
            attention(0)

            dve.wait_ge(lg_ps, 1)
            link(nc.vector.tensor_copy(lg[:], ps[:, 6, 0:64].rearrange("p (b e) -> p b e", e=E)))
            first_max(lg, m1, oh).then_inc(oh_rdy, 1)
            dve.wait_ge(cum_ps, 1)
            link(nc.vector.tensor_scalar(tiles_i[:], ps[:, 7, 64:72], float(P - 1), None, ALU.add))
            link(nc.vector.tensor_scalar(tiles_i[:], tiles_i[:], 7, None, ALU.logical_shift_right))
            link(nc.vector.tensor_copy(tiles_f[:], tiles_i[:]))
            link(nc.vector.tensor_tensor(upsel[:], upto[:], tiles_f[:].unsqueeze(1).to_broadcast([P, E, E]), ALU.mult))
            link(nc.vector.tensor_reduce(ends[:], upsel[:], axis=AX, op=ALU.add))
            link(nc.vector.tensor_tensor(base[:], ends[:], tiles_f[:], ALU.subtract))
            link(nc.vector.tensor_scalar(base[:], base[:], float(P), None, ALU.mult))
            link(nc.vector.tensor_tensor(oh2[:], ps[:, 7, 0:64].rearrange("p (b e) -> p b e", e=E),
                                         base[:].unsqueeze(1).to_broadcast([P, B, E]), ALU.add))
            link(nc.vector.tensor_tensor(oh2[:], oh2[:], oh[:], ALU.mult))
            link(nc.vector.tensor_reduce(slot_f[:], oh2[:], axis=AX, op=ALU.add))
            nc.vector.tensor_copy(slot_i[:], slot_f[:]).then_inc(slot_rdy, 1)
            link(nc.vector.tensor_tensor(cmp[:], ends[:].unsqueeze(1).to_broadcast([P, TILES, E]),
                                         tile_no[:].unsqueeze(2).to_broadcast([P, TILES, E]), ALU.is_le))
            link(nc.vector.tensor_reduce(eid_f[:], cmp[:], axis=AX, op=ALU.add))
            nc.vector.tensor_scalar(eid[:], eid_f[:], float(E - 1), None, ALU.min).then_inc(eid_rdy, 1)

            parts(1, True, 4)
            v_evac(1, 6)
            nc.vector.tensor_reduce(ctxsum[:], ctxT[:].rearrange("p (b m) -> p b m", m=M), axis=AX,
                                    op=ALU.add).then_inc(guard_in, 1)

            def xsT_evac(t):
                dve.wait_ge(xsT_ps, t + 1)
                if t >= 2:
                    dve.wait_ge(h_ps, t - 1)
                nc.vector.tensor_copy(xsT[:, t % 2, :], ps[:, 2, 0:P]).then_inc(xsT_sb, 1)

            def y_evac(t):
                dve.wait_ge(yt_ps, t + 1)
                if t >= 2:
                    dve.wait_ge(y_out[t % 2], 16 * (t // 2))
                nc.vector.tensor_copy(ys[:, t % 2, :], ps[:, 3, 0:D]).then_inc(yt_sb, 1)

            xsT_evac(0)
            for t in range(TILES):
                if t + 1 < TILES:
                    xsT_evac(t + 1)
                dve.wait_ge(h_relu, t + 1)
                if t >= 2:
                    dve.wait_ge(yt_ps, t - 1)
                nc.vector.tensor_tensor(h2[:, t % 2, :], hr[:, t % 2, :], hr[:, t % 2, :], ALU.mult).then_inc(h_sq, 1)
                if t >= 1:
                    y_evac(t - 1)
            y_evac(TILES - 1)

            for half in range(2):
                for b in range(4 * half, 4 * half + 4):
                    dve.wait_ge(gathered[b], 16)
                    ins = nc.vector.tensor_tensor(xr[:, b, :], xr[:, b, :], yg[:, b, :], ALU.add)
                link(ins)
                ln_stats(2, half)
            ln_normalise(2, 0)
            ln_normalise(2, 1)
            parts(1, False, 0)
            attention(1)
            dve.wait_ge(lg1_ps, 1)
            link(nc.vector.tensor_tensor(lg[:], ps[:, 6, 0:64].rearrange("p (b e) -> p b e", e=E),
                                         wcol(1, "bg").unsqueeze(1).to_broadcast([P, B, E]), ALU.add))
            link(nc.vector.tensor_reduce(m1[:], lg[:], axis=AX, op=ALU.max))
            nc.vector.tensor_tensor(lg[:], lg[:], m1[:].unsqueeze(2).to_broadcast([P, B, E]), ALU.subtract).then_inc(lg1_sub, 1)
            dve.wait_ge(lg1_exp, 1)
            link(nc.vector.tensor_reduce(gsum[:], pr[:], axis=AX, op=ALU.add))
            link(nc.vector.reciprocal(gsum[:], gsum[:]))
            link(nc.vector.tensor_tensor(pr[:], pr[:], gsum[:].unsqueeze(2).to_broadcast([P, B, E]), ALU.mult))
            link(first_max(pr, m1, oh2))
            link(nc.vector.scalar_tensor_tensor(p2[:], oh2[:], -2.0, pr[:], ALU.mult, ALU.add))
            link(first_max(p2, m2, gates))
            link(nc.vector.tensor_tensor(gates[:], gates[:], oh2[:], ALU.add))
            link(nc.vector.tensor_tensor(gates[:], gates[:], pr[:], ALU.mult))
            link(nc.vector.tensor_tensor(gsum[:], m1[:], m2[:], ALU.add))
            link(nc.vector.tensor_scalar(gsum[:], gsum[:], GATE_EPS, None, ALU.add))
            link(nc.vector.reciprocal(gsum[:], gsum[:]))
            ins = nc.vector.tensor_tensor(gates[:], gates[:], gsum[:].unsqueeze(2).to_broadcast([P, B, E]), ALU.mult)
            ins.then_inc(gates_rdy, 1)
            dve.wait_ge(gates_rdy, 1)
            for e in range(E):
                for half in range(2):
                    dve.wait_ge(dn_ps, 2 * e + half + 1)
                    if e > 0:
                        dve.wait_ge(x_exp, 2 * (e - 1) + half + 1)
                    for i in range(4):
                        b = 4 * half + i
                        ins = nc.vector.scalar_tensor_tensor(xr[:, b, :], ps[:, 4 + half, 128 * i:128 * i + 128],
                                                             gates[:, b, e:e + 1], xr[:, b, :], ALU.mult, ALU.add)
                    ins.then_inc(x_exp, 1)
                if e == 5:
                    dve.wait_ge(b2_ps, 1)
                    dve.wait_ge(x_exp, 2 * e + 2)
                    link(nc.vector.tensor_tensor(xr[:].rearrange("p b d -> p (b d)"),
                                                 ps[:, 6:8, :].rearrange("p a n -> p (a n)"),
                                                 xr[:].rearrange("p b d -> p (b d)"), ALU.add))

        @block.tensor
        def _(pe):
            mm = nc.tensor.matmul

            def k_proj(layer, bank):
                for i in range(8):
                    half, k = i // 4, i % 4
                    if i >= 4:
                        pe.wait_ge(k_sb, 8 * layer + i - 3)
                    mm(ps[:, bank + k, :], wcol(layer, "wk")[0:DC, P * k:P * k + P],
                       ctxT[:, 512 * half:512 * half + 512], start=True, stop=True).then_inc(k_ps, 1)

            def v_proj(layer, bank):
                for b in range(B):
                    ins = mm(ps[:, bank + b // 4, 128 * (b % 4):128 * (b % 4) + 128], ctxT[:, M * b:M * b + M],
                             wcol(layer, "wv")[0:DC, :], start=True, stop=True)
                ins.then_inc(v_ps, 1)

            def ln_transpose(k):
                for half in range(2):
                    pe.wait_ge(ln_norm, 2 * k + half + 1)
                    for i in range(4):
                        ins = nc.tensor.transpose(ps[:, 4 + half, 128 * i:128 * i + 128], xn[:, 4 * half + i, :], ident[:])
                    ins.then_inc(ln_tr, 1)

            def q_proj(layer):
                for i in range(8):
                    half, k = i // 4, i % 4
                    if k == 0:
                        pe.wait_ge(ln_xT, 4 * layer + half + 1)
                    if i >= 4:
                        pe.wait_ge(q_sb, 8 * layer + i - 3)
                    mm(ps[:, k, :], wcol(layer, "wq")[:, P * k:P * k + P], xT[:, 512 * half:512 * half + 512],
                       start=True, stop=True).then_inc(q_ps, 1)

            def attention(layer):
                def scores(b, u):
                    if b % 4 == 0 and u == 0:
                        pe.wait_ge(q_sb, 8 * layer + 4 * (b // 4) + 4)
                        if layer == 0:
                            pe.wait_ge(kmask_dve, b // 4 + 1)
                            pe.wait_ge(kmask_act, b // 4 + 1)
                    if b > 0:
                        pe.wait_ge(s_sub, BU(layer, b - 1, u))
                    for i in range(2):
                        k = 2 * u + i
                        ins = mm(ps[:, k, :], qk4[:, k, L * b:L * b + L],
                                 kmask[:, k, b, :, :].rearrange("p g m -> p (g m)"), start=True, stop=True)
                    ins.then_inc(s_ps, 1)

                def p_transpose(b, k):
                    pe.wait_ge(p_rdy, BU(layer, b, k // 2))
                    if b > 0 or k >= 2:
                        pe.wait_ge(pt_sb, BK(layer, b, k) - 2)
                    for g in range(4):
                        at = 512 * (k % 2) + 128 * g
                        ins = nc.tensor.transpose(ps[:, 4 + k % 2, 128 * g:128 * g + 128],
                                                  S_sb[:, b % 2, k // 2, at:at + 128], ident[:])
                    ins.then_inc(pt_ps, 1)

                def values(b, k):
                    pe.wait_ge(pt_sb, BK(layer, b, k))
                    if b == 0 and k == 0:
                        pe.wait_ge(v_sb, layer + 1)
                    if b > 0 and k == 0:
                        pe.wait_ge(o_sb, layer * B + b)
                    c, j = k // 2, k % 2
                    for g in range(4):
                        ins = mm(ps[32 * g:32 * g + 32, 6, 128 * c:128 * c + 128], vaug[:, b, 4 * k + g, :],
                                 PT[:, k, 128 * g:128 * g + 128], start=(j == 0), stop=(j == 1),
                                 tile_position=(0, 32 * g))
                    ins.then_inc(o_ps, 1)

                def o_transpose(b):
                    pe.wait_ge(o_sb, BB(layer, b))
                    if layer * B + b > 0:
                        pe.wait_ge(ot_sb, layer * B + b)
                    for c in range(2):
                        ins = nc.tensor.transpose(ps[:, 7, 128 * c:128 * c + 128], osb[:, b % 2, 128 * c:128 * c + 128], ident[:])
                    ins.then_inc(t_ps, 1)

                def a_transpose(b):
                    pe.wait_ge(att_sb, BB(layer, b))
                    nc.tensor.transpose(ps[:, 7, 256:384], att[:, b % 2, :], ident[:]).then_inc(a_ps, 1)

                def out_proj(half):
                    pe.wait_ge(s_wr, 16)
                    pe.wait_ge(s_sub, BU(layer, B - 1, 0))
                    pe.wait_ge(ot_sb, BB(layer, 4 * half + 3))
                    for i in range(4):
                        ins = mm(ps[:, half, 128 * i:128 * i + 128], OT[:, 4 * half + i, :], wcol(layer, "wo"),
                                 start=True, stop=True)
                    ins.then_inc(y_ps, 1)

                scores(0, 0)
                scores(0, 1)
                if layer == 1:
                    pe.wait_ge(guard_in, 1)
                    mm(ps[:, 7, B:2 * B], wcol(1, "wv")[0:DC, :], ctxsum[:], start=True, stop=True)
                    pe.wait_ge(guard_cnt, 1)
                    mm(ps[:, 7, 16:17], ones[:], nan_rows[:], start=True, stop=True).then_inc(guard_tot, 1)
                for b in range(B + 1):
                    if b + 1 < B:
                        scores(b + 1, 0)
                    if b < B:
                        p_transpose(b, 0)
                        p_transpose(b, 1)
                        values(b, 0)
                    if b + 1 < B:
                        scores(b + 1, 1)
                    if b > 0:
                        o_transpose(b - 1)
                    if b < B:
                        p_transpose(b, 2)
                        values(b, 1)
                        p_transpose(b, 3)
                        values(b, 2)
                    if b > 0:
                        a_transpose(b - 1)
                    if b < B:
                        values(b, 3)
                    if b == B - 1:
                        out_proj(0)
                out_proj(1)

            pe.wait_ge(s_ctx, 16)
            pe.wait_ge(s_wa, 16)
            k_proj(0, 0)
            v_proj(0, 6)
            pe.wait_ge(pool_const, CONSTS)
            ln_transpose(0)
            pe.wait_ge(k_sb, 8)
            pe.wait_ge(s_wq, 16)
            q_proj(0)
            pe.wait_ge(v_sb, 1)
            pe.wait_ge(q_sb, 8)
            attention(0)

            ln_transpose(1)
            for b in range(B):
                if b % 4 == 0:
                    pe.wait_ge(ln_xT, 3 + b // 4)
                ins = mm(ps[:, 6, E * b:E * b + E], xT[:, L * b:L * b + L], wcol(0, "rw"), start=True, stop=True)
            ins.then_inc(lg_ps, 1)
            pe.wait_ge(oh_rdy, 1)
            mm(ps[:, 7, 0:B * E], before[:], oh[:].rearrange("p b e -> p (b e)"), start=True, stop=False)
            for b in range(B - 1):
                mm(ps[:, 7, E * (b + 1):B * E].rearrange("p (b e) -> p b e", e=E), ones_bf[:],
                   oh[:, b:b + 1, :].to_broadcast([P, B - 1 - b, E]), start=False, stop=(b == B - 2))
            for b in range(B):
                ins = mm(ps[:, 7, B * E:B * E + E], ones_bf[:], oh[:, b, :], start=(b == 0), stop=(b == B - 1))
            ins.then_inc(cum_ps, 1)

            pe.wait_ge(slot_rdy, 1)
            k_proj(1, 4)
            pe.wait_ge(k_sb, 16)
            v_proj(1, 6)

            def xs_transpose(t):
                for i, (lo, _) in enumerate(XS_PARTS):
                    if t == lo:
                        pe.wait_ge(xs_in[i], 16)
                if t >= 1:
                    pe.wait_ge(xsT_sb, t)
                nc.tensor.transpose(ps[:, 2, 0:P], xs[:, t, :], ident[:]).then_inc(xsT_ps, 1)

            def up(t):
                pe.wait_ge(xsT_sb, t + 1)
                pe.wait_ge(fc_rdy, t + 1)
                if t >= 2:
                    pe.wait_ge(h_relu, t - 1)
                for c in range(C0):
                    ins = mm(ps[:, t % 2, P * c:P * c + P], fcb[:, t % 2, P * c:P * c + P], xsT[:, t % 2, :],
                             start=True, stop=True)
                ins.then_inc(h_ps, 1)

            def down(t):
                expert = pe.value_load(eid[0:1, t:t + 1], min_val=0, max_val=E - 1)
                pe.wait_ge(h_sq, t + 1)
                if t >= 1:
                    pe.wait_ge(yt_sb, t)
                for c in range(C0):
                    ins = mm(ps[:, 3, 0:D], h2[:, t % 2, P * c:P * c + P],
                             proj[:, bass.ds(expert, 1), c, :].rearrange("p a d -> p (a d)"),
                             start=(c == 0), stop=(c == C0 - 1))
                ins.then_inc(yt_ps, 1)

            xs_transpose(0)
            pe.wait_ge(eid_rdy, 1)
            for t in range(TILES):
                if t + 1 < TILES:
                    xs_transpose(t + 1)
                up(t)
                if t >= 1:
                    down(t - 1)
            down(TILES - 1)

            pe.wait_ge(v_sb, 2)
            ln_transpose(2)
            q_proj(1)
            pe.wait_ge(kmask_dma, 16 * H)
            pe.wait_ge(q_sb, 16)
            attention(1)
            ln_transpose(3)
            for b in range(B):
                if b % 4 == 0:
                    pe.wait_ge(ln_xT, 7 + b // 4)
                ins = mm(ps[:, 6, E * b:E * b + E], xT[:, L * b:L * b + L], wcol(1, "wg"), start=True, stop=True)
            ins.then_inc(lg1_ps, 1)

            def expert_up(e, half):
                if half == 0:
                    pe.wait_ge(s_w12[e % 2], 32 * (e // 2 + 1))
                if e > 0:
                    pe.wait_ge(hT_rdy, (2 * (e - 1) + half + 1) * C1)
                for c in range(C1):
                    mm(ps[:, 2 * half + c, :], w1[:, e % 2, P * c:P * c + P], xT[:, 512 * half:512 * half + 512],
                       start=True, stop=True).then_inc(up_ps, 1)

            def expert_down(e, half):
                pe.wait_ge(hT_rdy, (2 * e + half + 1) * C1)
                if e > 0:
                    pe.wait_ge(x_exp, 2 * (e - 1) + half + 1)
                for i in range(4):
                    for c in range(C1):
                        ins = mm(ps[:, 4 + half, P * i:P * i + P], hT[:, half, c, P * i:P * i + P], w2[:, e % 2, c, :],
                                 start=(c == 0), stop=(c == C1 - 1))
                ins.then_inc(dn_ps, 1)

            def gates_transpose():
                pe.wait_ge(gates_rdy, 1)
                for b in range(B):
                    ins = nc.tensor.transpose(ps[0:E, 6 + b // 4, L * (b % 4):L * (b % 4) + L], gates[:, b, :], ident[:])
                ins.then_inc(gT_ps, 1)

            def gated_b2():
                pe.wait_ge(gT_sb, 1)
                pe.wait_ge(s_b2, 16)
                for b in range(B):
                    ins = mm(ps[:, 6 + b // 4, D * (b % 4):D * (b % 4) + D], gT[:, b, :], b2[:], start=True, stop=True)
                ins.then_inc(b2_ps, 1)

            expert_up(0, 0)
            expert_up(0, 1)
            for e in range(E):
                for half in range(2):
                    expert_down(e, half)
                    if e + 1 < E:
                        expert_up(e + 1, half)
                if e == 1:
                    gates_transpose()
                if e == 3:
                    gated_b2()


_OUT = (8, 128, 128)


def kernel(**inputs):
    import numpy as np
    import concourse.bacc as bacc
    from concourse.bass_utils import run_bass_kernel_spmd

    def get(name):
        return np.asarray(inputs[name])

    def rows(a):
        out = np.zeros((P, a.shape[1]), a.dtype)
        out[:a.shape[0]] = a
        return out

    def quads(a):
        a = a.reshape(a.shape[0], 4, 1, 32)
        return np.broadcast_to(a, (a.shape[0], 4, 4, 32)).reshape(a.shape[0], 512)

    def bias4(a, rows_of=(0, 1, 2, 3)):
        out = np.zeros((4, 32, 4), a.dtype)
        for t in rows_of:
            out[t] = a.reshape(4, 32).T
        return out.reshape(P, 4)

    def spread(a):
        return np.broadcast_to(a[None, :], (P, a.shape[0]))

    vperm = np.array([DH * (8 * c + 4 * j + g) + d for c in range(2) for g in range(4) for j in range(2) for d in range(DH)])
    kv = get("L0_xattn_Wkv").reshape(H, 2, DH, DC)
    bkv = get("L0_xattn_bkv").reshape(H, 2, DH)
    layer0 = dict(
        wk=quads(rows(kv[:, 0].reshape(D, DC).T)), wv=rows(kv[:, 1].reshape(D, DC)[vperm].T),
        wq=quads(get("L0_xattn_Wq").T), bq=bias4(get("L0_xattn_bq")), bql=bias4(get("L0_xattn_bq"), (2, 3)),
        bk=bias4(bkv[:, 0].reshape(D)), bkl=bias4(bkv[:, 0].reshape(D), (1, 3)), bv=bkv[:, 1].reshape(D)[vperm][:, None])
    rest = dict(
        wo0=get("L0_xattn_Wo").T[vperm], bo0=spread(get("L0_xattn_bo")), rw=get("L0_ffn_router_w").T,
        wk=quads(rows(get("L1_xattn_Wk"))), wv=rows(get("L1_xattn_Wv")[:, vperm]), wq=quads(get("L1_xattn_Wq")),
        bq=bias4(get("L1_xattn_bq")), bql=bias4(get("L1_xattn_bq"), (2, 3)),
        bk=bias4(get("L1_xattn_bk")), bkl=bias4(get("L1_xattn_bk"), (1, 3)), bv=get("L1_xattn_bv")[vperm][:, None],
        wo1=get("L1_xattn_Wo")[vperm], bo1=spread(get("L1_xattn_bo")), wg=get("L1_ffn_Wg"), bg=spread(get("L1_ffn_bg")))
    arrays = dict(
        x=get("x").reshape(N, D),
        ctxT=get("ctx_768").reshape(B * M, DC).T,
        wa=np.concatenate([layer0[n] for n in A_COLS], axis=1),
        wr=np.concatenate([rest[n] for n in R_COLS], axis=1),
        fc=get("L0_ffn_expert_fc").transpose(1, 0, 2),
        proj=get("L0_ffn_expert_proj").reshape(E, D, C0, P).transpose(3, 0, 2, 1),
        w1=np.concatenate([get("L1_ffn_W1"), get("L1_ffn_b1").reshape(E, C1, P).transpose(0, 2, 1)], axis=2),
        w2=get("L1_ffn_W2").reshape(E, C1, P, D).transpose(0, 2, 1, 3),
        b2=get("L1_ffn_b2"))
    nc = bacc.Bacc("TRN2", target_bir_lowering=False, num_devices=1)
    in_map, args = {}, []
    for name, a in arrays.items():
        in_map["in_" + name] = np.ascontiguousarray(a)
        args.append(nc.dram_tensor("in_" + name, in_map["in_" + name].shape, mybir.dt.from_np(in_map["in_" + name].dtype), kind="ExternalInput").ap())
    out = nc.dram_tensor("out", (N, D), mybir.dt.float32, kind="ExternalOutput").ap()
    build(nc, *args, out)
    result = run_bass_kernel_spmd(nc, [in_map], core_ids=[0])
    return result.results[0]["out"].reshape(_OUT)
```
